# Optimizing a Trainium2 kernel written in Bass

```python
import numpy as np
import jax
import jax.numpy as jnp

def _softmax(x, axis=-1):
    return jax.nn.softmax(x, axis=axis)

def _gelu(x):
    return jax.nn.gelu(x, approximate=True)

def _silu(x):
    return jax.nn.silu(x)

def _sigmoid(x):
    return jax.nn.sigmoid(x)

def _layernorm(x, axis=-1, eps=1e-05):
    m = jnp.mean(x, axis=axis, keepdims=True)
    v = jnp.var(x, axis=axis, keepdims=True)
    return (x - m) / jnp.sqrt(v + eps)

def _scatter_add(tgt, idx, src, axis=0):
    return tgt.at[idx].add(src)

def _segment_sum(src, seg, n):
    return jax.ops.segment_sum(src, seg, n)
kernel_name = 'mk_metaformer_d1_conv_nchw512_r4_29a44b'

def setup_inputs(seed: int=0):
    np.random.seed(seed)
    _w = jnp.asarray

    def _rec_inputs():
        import jax
        import jax.numpy as jnp
        _gk = jax.random.key(seed)
        x = -0.0003482 + 1 * jax.random.normal(jax.random.fold_in(_gk, 1), (4, 128, 24, 24), jnp.float32)
        return x
    x = _rec_inputs()

    def _L0_conv_setup():
        import jax, jax.numpy as jnp
        import numpy as np
        HEADS = 8
        DIM = 128
        SCALE = (DIM // HEADS) ** (-0.5)
        key = jax.random.key(seed)
        k1, k2, k3, k4 = jax.random.split(key, 4)
        B, C, H, W = (4, DIM, 24, 24)
        x = jax.random.normal(k1, (B, C, H, W), dtype=jnp.float32)
        w_qkv = jax.random.normal(k2, (3 * DIM, DIM), dtype=jnp.float32) * DIM ** (-0.5)
        w_out = jax.random.normal(k3, (DIM, DIM), dtype=jnp.float32) * DIM ** (-0.5)
        b_out = jax.random.normal(k4, (DIM,), dtype=jnp.float32) * 0.01
        return {'x': x, 'w_qkv': w_qkv, 'w_out': w_out, 'b_out': b_out}
    _L0_conv_all = _L0_conv_setup()
    _L0_conv_in = {k: v for k, v in _L0_conv_all.items() if k in ('w_qkv', 'w_out', 'b_out')}
    del _L0_conv_all

    def _L0_ffn_setup():
        import jax, jax.numpy as jnp
        import numpy as np
        K = 2
        key = jax.random.key(seed)
        k1, k2, k3, k4 = jax.random.split(key, 4)
        B, L, D, H, E = (8, 256, 128, 256, 16)
        x = jax.random.normal(k1, (B, L, D), dtype=jnp.float32)
        W_gate = jax.random.normal(k2, (D, E), dtype=jnp.float32) * 0.02
        W1 = jax.random.normal(k3, (E, D, H), dtype=jnp.float32) * 0.02
        W2 = jax.random.normal(k4, (E, H, D), dtype=jnp.float32) * 0.02
        return {'x': x, 'W_gate': W_gate, 'W1': W1, 'W2': W2}
    _L0_ffn_all = _L0_ffn_setup()
    _L0_ffn_in = {k: v for k, v in _L0_ffn_all.items() if k in ('W_gate', 'W1', 'W2')}
    del _L0_ffn_all
    return {'x': x, 'L0_conv_w_qkv': _L0_conv_in['w_qkv'], 'L0_conv_w_out': _L0_conv_in['w_out'], 'L0_conv_b_out': _L0_conv_in['b_out'], 'L0_ffn_W_gate': _L0_ffn_in['W_gate'], 'L0_ffn_W1': _L0_ffn_in['W1'], 'L0_ffn_W2': _L0_ffn_in['W2']}

def reference(x, L0_conv_w_qkv, L0_conv_w_out, L0_conv_b_out, L0_ffn_W_gate, L0_ffn_W1, L0_ffn_W2):
    import jax
    import jax.numpy as jnp

    def _L0_conv_ref(x, w_qkv, w_out, b_out):
        import jax, jax.numpy as jnp
        import numpy as np
        HEADS = 8
        DIM = 128
        SCALE = (DIM // HEADS) ** (-0.5)
        b, c, h, w = x.shape
        heads = HEADS
        d = c // heads
        qkv = jnp.einsum('bchw,oc->bohw', x, w_qkv)
        qkv = qkv.reshape(b, 3, heads, d, h, w)
        qkv = jnp.transpose(qkv, (1, 0, 2, 4, 5, 3))
        q, k, v = (qkv[0], qkv[1], qkv[2])
        dots = jnp.einsum('bhxid,bhxjd->bhxij', q, k) * SCALE
        attn = jax.nn.softmax(dots, axis=-1)
        out = jnp.einsum('bhxij,bhxjd->bhxid', attn, v)
        out = jnp.transpose(out, (0, 1, 4, 2, 3)).reshape(b, heads * d, h, w)
        out = jnp.einsum('bchw,oc->bohw', out, w_out) + b_out[None, :, None, None]
        return out

    def _L0_ffn_ref(x, W_gate, W1, W2):
        import jax, jax.numpy as jnp
        import numpy as np
        K = 2
        B, L, D = x.shape
        E = W_gate.shape[1]
        xf = x.reshape(-1, D)
        T = xf.shape[0]
        probs = jax.nn.softmax(xf @ W_gate, axis=-1)
        top_g, top_i = jax.lax.top_k(probs, K)
        gates = jnp.zeros((T, E), dtype=x.dtype).at[jnp.arange(T)[:, None], top_i].set(top_g)

        def step(y, params):
            W1e, W2e, ge = params
            h = jax.nn.gelu(xf @ W1e, approximate=False)
            return (y + ge[:, None] * (h @ W2e), None)
        y0 = jnp.zeros((T, D), dtype=x.dtype)
        y, _ = jax.lax.scan(step, y0, (W1, W2, gates.T))
        return y.reshape(B, L, D)

    def _gn(v, G=32, eps=1e-05):
        B_, C_, H_, W_ = v.shape
        g = v.reshape(B_, G, C_ // G, H_, W_)
        m = jnp.mean(g, axis=(2, 3, 4), keepdims=True)
        s = jnp.var(g, axis=(2, 3, 4), keepdims=True)
        return ((g - m) / jnp.sqrt(s + eps)).reshape(v.shape)

    def _ln_c(v, eps=1e-06):
        m = jnp.mean(v, axis=1, keepdims=True)
        s = jnp.var(v, axis=1, keepdims=True)
        return (v - m) / jnp.sqrt(s + eps)

    def _ln_t(v, eps=1e-05):
        m = jnp.mean(v, axis=-1, keepdims=True)
        s = jnp.var(v, axis=-1, keepdims=True)
        return (v - m) / jnp.sqrt(s + eps)

    def _to_tokens(v):
        B_, C_, H_, W_ = v.shape
        return v.reshape(B_, C_, H_ * W_).transpose(0, 2, 1)

    def _from_tokens(t, like):
        B_, C_, H_, W_ = like.shape
        return t.transpose(0, 2, 1).reshape(B_, C_, H_, W_)
    x = x + _L0_conv_ref(_ln_c(x), L0_conv_w_qkv, L0_conv_w_out, L0_conv_b_out)
    t = _to_tokens(x)
    t = t + _L0_ffn_ref(_ln_t(t), L0_ffn_W_gate, L0_ffn_W1, L0_ffn_W2)
    x = _from_tokens(t, x)
    return x

_drawn_inputs = setup_inputs


def setup_inputs(seed=0):
    import zlib

    import numpy as np

    out = dict(_drawn_inputs(seed))
    spreads = {}
    factors = {'L0_conv_b_out': 5.786, 'L0_ffn_W_gate': 8.0, 'L0_ffn_W1': 8.0, 'L0_ffn_W2': 8.0}
    for name, (base, spread) in spreads.items():
        noise = np.random.default_rng([zlib.crc32(name.encode()), seed]).standard_normal(out[name].shape)
        drawn = base * np.exp(spread * noise) if base else spread * noise
        out[name] = jnp.asarray(drawn.astype(out[name].dtype))
    for name, factor in factors.items():
        out[name] = (out[name] * factor).astype(out[name].dtype)
    return out
```

```python
from contextlib import ExitStack

import numpy as np
import concourse.bass as bass
from concourse import mybir

F32 = mybir.dt.float32
BF16 = mybir.dt.bfloat16
I32 = mybir.dt.int32
U32 = mybir.dt.uint32
ALU = mybir.AluOpType
ACT = mybir.ActivationFunctionType
AX = mybir.AxisListType

P = 128
B, C, H, W = 4, 128, 24, 24
HEADS = 8
HD = C // HEADS
SCALE = HD ** -0.5
E = 16
HID = 256
NHALF = HID // P
EPS_C = 1e-6
EPS_T = 1e-5
TOK = B * H * W

RG = 4
WP = 32
GT = RG * W
NG = 3
CT = NG * GT
CR = NG * RG
NCH = TOK // CT
HF = 2
HQ = HEADS // HF
NP = HEADS // 2
TOPK = 2

TS = 128
CAP = TOK + TS
RW = C + 4
ID, GATE = C, C + 1
NT = (TOPK * TOK + E * (TS - 1)) // TS + 1
AHEAD = 4
NTAB = NT + AHEAD
YROWS = TOPK * TOK
SKIP = 8192


def build(nc, x, w_qkv, w_out, b_out, w_gate, w1, w2, out):
    x_v = x.rearrange("b c h w -> c b (h w)")
    out_v = out.rearrange("b c h w -> c b (h w)")
    slots = nc.dram_tensor("slots", (E * CAP, RW), F32, kind="Internal").ap()
    y_rows = nc.dram_tensor("y_rows", (YROWS, C), F32, kind="Internal").ap()

    ctx = ExitStack()
    with ctx:
        def sb(name, shape, dt=F32):
            return ctx.enter_context(nc.sbuf_tensor(name, shape, dt))

        def sem(name):
            return ctx.enter_context(nc.semaphore(name))

        x_sb = sb("x_sb", [P, TOK])
        t_sb = sb("t_sb", [P, TOK])
        wqkv_sb = sb("wqkv_sb", [P, 3, C])
        wout_sb = sb("wout_sb", [P, C])
        wT = sb("wT", [P, 4, C])
        bo = sb("bo", [P, 1])
        wg = sb("wg", [P, E])
        wgc = sb("wgc", [P, E])
        w1_sb = sb("w1_sb", [P, E * HID])
        w2_sb = sb("w2_sb", [P, E * NHALF * C])
        ident = sb("ident", [P, P])
        cmat = sb("cmat", [P, P])
        avg = sb("avg", [P, P])
        tri = sb("tri", [GT, GT], BF16)
        ones = sb("ones", [GT, P], BF16)
        hmask = sb("hmask", [P, HEADS])
        kmask = sb("kmask", [P, HQ])
        hscale = sb("hscale", [P, HF, HQ])
        pmask = sb("pmask", [P, 2])
        iota_e = sb("iota_e", [P, E])
        ebase = sb("ebase", [P, E])
        ids = sb("ids", [GT, TOPK, NG])
        chunk_step = sb("chunk_step", [GT, TOPK, NG])
        carrier = sb("carrier", [1, 1])
        zero_c = sb("zero_c", [P, 1])
        eps_c = sb("eps_c", [P, 1])
        eps_t = sb("eps_t", [P, 1])
        lnv = sb("lnv", [P, CT])
        lnv2 = sb("lnv2", [GT, NG])
        pad_rows = sb("pad_rows", [P, RW])
        padid = sb("padid", [P, 1])

        sq = [sb(f"sq{i}", [P, CT]) for i in range(2)]
        rstd = sb("rstd", [P, CT])
        xn = [sb(f"xn{i}", [P, CR * WP]) for i in range(2)]
        qs = [sb(f"qs{i}", [P, CR * WP]) for i in range(2)]
        km = [sb(f"km{i}", [P, HQ, CT]) for i in range(2)]
        vs = [sb(f"vs{i}", [P, NG * C]) for i in range(2)]
        mx = sb("mx", [P, HF * NG * HQ])
        den = sb("den", [P, HF * NG * HQ])
        rden = sb("rden", [P, HF * NG * HQ])
        es = [sb(f"es{i}", [P, HF * NG * HQ, W]) for i in range(2)]
        ex = [sb(f"ex{i}", [P, HF * NG * HQ, WP]) for i in range(2)]
        exT = [sb(f"exT{i}", [P, HF * NG * HQ, WP]) for i in range(2)]
        av0 = sb("av0", [P, CT])
        o_sb = [sb(f"o_sb{i}", [P, CT]) for i in range(2)]
        tc = [sb(f"tc{i}", [P, CT]) for i in range(2)]
        bst = sb("bst", [GT, NG, 6])
        bmv = sb("bmv", [GT, NG, 2])
        rstd2 = sb("rstd2", [GT, NG])
        nmr = sb("nmr", [GT, NG])
        rows = [sb(f"rows{i}", [GT, TOPK, NG, RW]) for i in range(2)]
        lg = sb("lg", [GT, NG, E])
        m8 = sb("m8", [GT, NG, 8])
        i8 = sb("i8", [GT, NG, 8], U32)
        idx = sb("idx", [GT, TOPK, NG])
        nm0 = sb("nm0", [GT, NG])
        dm = sb("dm", [GT, NG])
        junk = sb("junk", [GT, NG, E])
        esum = sb("esum", [GT, NG])
        e2 = sb("e2", [GT, NG])
        oh = sb("oh", [GT, TOPK, NG * E])
        mt = sb("mt", [GT, NG, E], BF16)
        msum = sb("msum", [GT, E])
        macc = sb("macc", [GT, E])
        maccb = sb("maccb", [GT, E], BF16)
        posb = sb("posb", [GT, NG * E])
        prod = sb("prod", [GT, TOPK, NG * E])
        destf = sb("destf", [GT, TOPK * NG])
        dest = [sb(f"dest{i}", [GT, TOPK * NG], U32) for i in range(2)]
        rg = sb("rg", [GT, NG])

        iota_t = sb("iota_t", [P, NTAB])
        iota_p = sb("iota_p", [P, 1])
        cnt = sb("cnt", [P, E])
        nt_i = sb("nt_i", [P, E], I32)
        nt_f = sb("nt_f", [P, E])
        ct_f = sb("ct_f", [P, E])
        one_e = sb("one_e", [P, E])
        past = sb("past", [P, NTAB, E + 1])
        tw = sb("tw", [P, NTAB, E])
        first = sb("first", [P, NTAB])
        c_t = sb("c_t", [P, NTAB])
        e_t = sb("e_t", [P, NTAB])
        j128 = sb("j128", [P, NTAB])
        start = sb("start", [P, NTAB])
        skip = sb("skip", [P, NTAB])
        e_c = sb("e_c", [P, NTAB])
        rowoff = sb("rowoff", [P, NTAB], I32)
        woff = sb("woff", [P, NTAB], I32)

        xs = [sb(f"xs{i}", [P, RW]) for i in range(AHEAD)]
        xT = [sb(f"xT{i}", [P, TS]) for i in range(2)]
        h_sb = [sb(f"h_sb{i}", [P, HID]) for i in range(2)]
        hT = [sb(f"hT{i}", [P, HID]) for i in range(2)]
        y_sb = [sb(f"y_sb{i}", [P, C]) for i in range(AHEAD)]
        ret = [sb(f"ret{i}", [P, 1], U32) for i in range(AHEAD)]

        NY = TOK // P
        FB = 4
        YB = [(m, min(m + FB, NY)) for m in range(0, NY, FB)]
        yk = sb("yk", [P, TOPK, NY * C])
        ysum = sb("ysum", [P, NY * C])
        fin = x_sb

        ps = ctx.enter_context(nc.psum_tensor("ps", [P, 8 * 512], F32))

        def bank(i, n=512, p=P):
            return ps[0:p, i * 512:i * 512 + n]

        XC_K, VAR_Q, S0, AV0, V_B, PJ_B, TR_B, RT_B = 0, 1, 2, 4, 4, 5, 6, 7
        LG = ps[0:GT, RT_B * 512:RT_B * 512 + NG * E]
        POS = ps[0:GT, RT_B * 512 + 64:RT_B * 512 + 64 + NG * E]
        CNT = ps[0:P, RT_B * 512 + 128:RT_B * 512 + 128 + E]
        s_view = ps[:, S0 * 512:(S0 + 2) * 512].rearrange("p (f n) -> p f n", f=HF)[:, :, 0:NG * HQ * W] \
            .rearrange("p f (a j) -> p f a j", j=W)
        av_view = ps[:, AV0 * 512:(AV0 + 4) * 512].rearrange("p (r n) -> p r n", r=RG)[:, :, 0:2 * NG * W] \
            .rearrange("p r (a n) -> p r a n", a=2)

        s_cst = sem("s_cst")
        s_cstv = sem("s_cstv")
        s_free = sem("s_free")
        s_carrier = sem("s_carrier")
        s_masks = sem("s_masks")
        s_xin = [sem(f"s_xin{i}") for i in range(2)]
        s_win = sem("s_win")
        s_w1 = sem("s_w1")
        s_w2 = sem("s_w2")
        s_pre = sem("s_pre")
        s_wtp = sem("s_wtp")
        s_wt = sem("s_wt")
        s_v = sem("s_v")
        s_xc = sem("s_xc")
        s_sq = sem("s_sq")
        s_var = sem("s_var")
        s_xn = sem("s_xn")
        s_qp = sem("s_qp")
        s_kp = sem("s_kp")
        s_q = sem("s_q")
        s_km = sem("s_km")
        s_vp = sem("s_vp")
        s_vs = sem("s_vs")
        s_s = sem("s_s")
        s_sub = sem("s_sub")
        s_e = sem("s_e")
        s_et = sem("s_et")
        s_av = sem("s_av")
        s_av0 = sem("s_av0")
        s_o = sem("s_o")
        s_pj = sem("s_pj")
        s_t = sem("s_t")
        s_tcp = sem("s_tcp")
        s_tr = sem("s_tr")
        s_lg = sem("s_lg")
        s_st = sem("s_st")
        s_rows = sem("s_rows")
        s_m0 = sem("s_m0")
        s_mt = sem("s_mt")
        s_gx = sem("s_gx")
        s_pos = sem("s_pos")
        s_pb = sem("s_pb")
        s_macc = sem("s_macc")
        s_meta = sem("s_meta")
        s_scat = [sem(f"s_scat{i}") for i in range(2)]
        s_cnt = sem("s_cnt")
        s_tab = sem("s_tab")
        s_ld = [sem(f"s_ld{i}") for i in range(AHEAD)]
        s_trx = sem("s_trx")
        s_xT = sem("s_xT")
        s_h = sem("s_h")
        s_g = sem("s_g")
        s_th = sem("s_th")
        s_hT = sem("s_hT")
        s_yp = sem("s_yp")
        s_y = sem("s_y")
        s_ret = sem("s_ret")
        s_ysc = [sem(f"s_ysc{i}") for i in range(AHEAD)]
        s_yk = [sem(f"s_yk{i}") for i in range(len(YB))]
        s_ys = sem("s_ys")
        s_yt = sem("s_yt")
        s_fin = sem("s_fin")
        s_out = sem("s_out")

        s_rs, s_mx, s_den, s_rden, s_nrm, s_bst, s_bmv, s_rs2, s_lgs, s_m8, s_i8, s_idx, s_oh, s_ms, s_ma, \
            s_pr, s_df, s_rg, s_ids, s_lnv, s_lnv2 = [sem(f"s_{k}") for k in (
                "rs", "mx", "den", "rden", "nrm", "bst", "bmv", "rs2", "lgs", "m8", "i8", "idx", "oh", "ms",
                "ma", "pr", "df", "rg", "ids", "lnv", "lnv2")]

        NCST = 12
        CREDIT = 1
        TPI = 2
        FPI = AHEAD

        block = ctx.enter_context(nc.Block())

        @block.sync
        def _(sp):
            sp.dma_start(wqkv_sb[:, :, :], w_qkv.rearrange("(a o) c -> o a c", a=3)).then_inc(s_win, 16)
            sp.dma_start(x_sb[:, 0:TOK // B], x_v[:, 0, :]).then_inc(s_xin[0], 16)
            sp.dma_start(wout_sb[:, :], w_out).then_inc(s_win, 16)
            sp.dma_start(bo[:, :], b_out.rearrange("(c a) -> c a", a=1)).then_inc(s_win, 16)
            sp.dma_start(wg[:, :], w_gate).then_inc(s_win, 16)
            sp.dma_start(x_sb[:, TOK // B:].rearrange("c (b n) -> c b n", b=B - 1),
                         x_v[:, 1:, :]).then_inc(s_xin[1], 16)
            sp.wait_ge(s_cstv, 2)
            sp.dma_start(slots.rearrange("(e p) w -> p e w", e=E)[0:TS, :, :],
                         pad_rows[:, :].unsqueeze(1).broadcast_to([P, E, RW])).then_inc(s_pre, 16)
            sp.sem_inc(s_free, TPI)
            with sp.Fori(0, NCH // TPI) as i:
                for c in range(TPI):
                    sp.wait_ge(s_scat[c], i * (16 * TOPK * NG) + 16 * TOPK * NG)
                    sp.sem_inc(s_free, 1)
            sp.wait_ge(s_tab, 1)
            sp.wait_ge(s_pre, 16)
            sp.wait_ge(s_scat[0], 16 * TOPK * NG * NCH // 2)
            sp.wait_ge(s_scat[1], 16 * TOPK * NG * NCH // 2)
            for u in range(AHEAD):
                off = sp.value_load(rowoff[0:1, u:u + 1], min_val=0, max_val=E * CAP - TS)
                sp.dma_start(xs[u][:, :], slots[bass.DynSlice(off, TS), :]).then_inc(s_ld[u], 16)
            with sp.Fori(0, NT // FPI) as i:
                for u in range(FPI):
                    t = i * FPI + u
                    off = sp.value_load(rowoff[0:1, bass.DynSlice(t + AHEAD, 1)], min_val=0, max_val=E * CAP - TS)
                    sp.wait_ge(s_trx, t + 1 + CREDIT)
                    sp.wait_ge(s_ret, t + 1 + CREDIT)
                    sp.wait_ge(s_y, t + 1 + CREDIT)
                    sp.dma_start(xs[u][:, :], slots[bass.DynSlice(off, TS), :]).then_inc(s_ld[u], 16)
            for u in range(AHEAD):
                sp.wait_ge(s_ysc[u], 16 * (NT // FPI))
                sp.wait_ge(s_ld[u], 16 * (NT // FPI + 1))
            y_v = y_rows.rearrange("(k n p) d -> p k n d", k=TOPK, p=P)
            for b, (n0, n1) in enumerate(YB):
                for k in range(TOPK):
                    sp.dma_start(yk[:, k, n0 * C:n1 * C].rearrange("p (n d) -> p n d", d=C),
                                 y_v[:, k, n0:n1, :]).then_inc(s_yk[b], 16)
            for b in range(B):
                sp.wait_ge(s_fin, -(-(b + 1) * (TOK // B) // (FB * P)))
                sp.dma_start(out_v[:, b, :], fin[:, b * (TOK // B):(b + 1) * (TOK // B)]).then_inc(s_out, 16)
            sp.wait_ge(s_out, 16 * B)

        @block.gpsimd
        def _(pool):
            g = nc.gpsimd
            for free in (s_ids, s_carrier):
                pool.sem_inc(free, CREDIT)
            g.memset(chunk_step[:, :, :], float(CT))
            g.memset(ident[:, :], 0.0).then_inc(s_cst, 1)
            g.memset(tri[:, :], 0.0).then_inc(s_cst, 1)
            g.memset(hmask[:, :], 1.0).then_inc(s_cst, 1)
            pool.wait_ge(s_cst, 3)
            g.affine_select(out=ident[:, :], in_=ident[:, :], compare_op=ALU.not_equal, fill=1.0,
                            base=0, pattern=[[-1, P]], channel_multiplier=1).then_inc(s_cst, 1)
            g.affine_select(out=tri[:, :], in_=tri[:, :], compare_op=ALU.is_ge, fill=1.0,
                            base=0, pattern=[[-1, GT]], channel_multiplier=1).then_inc(s_cst, 1)
            g.affine_select(out=hmask[:, :], in_=hmask[:, :], compare_op=ALU.is_ge, fill=0.0,
                            base=0, pattern=[[-HD, HEADS]], channel_multiplier=1).then_inc(s_cst, 1)
            pool.wait_ge(s_cst, 6)
            g.affine_select(out=hmask[:, :], in_=hmask[:, :], compare_op=ALU.is_ge, fill=0.0,
                            base=HD - 1, pattern=[[HD, HEADS]], channel_multiplier=-1).then_inc(s_cst, 1)
            exact = dict(allow_small_or_imprecise_dtypes=True)
            g.iota(iota_e[:, :], pattern=[[1, E]], base=0, channel_multiplier=0, **exact).then_inc(s_cst, 1)
            g.iota(ebase[:, :], pattern=[[CAP, E]], base=0, channel_multiplier=0, **exact).then_inc(s_cst, 1)
            g.iota(ids[:, :, :], pattern=[[TOK, TOPK], [GT, NG]], base=0, channel_multiplier=1,
                   **exact).then_inc(s_cst, 1)
            g.iota(iota_t[:, :], pattern=[[1, NTAB]], base=0, channel_multiplier=0, **exact).then_inc(s_cst, 1)
            g.iota(iota_p[:, :], pattern=[[0, 1]], base=0, channel_multiplier=1, **exact).then_inc(s_cst, 1)
            pool.wait_ge(s_pre, 16)
            with pool.Fori(0, NCH // TPI) as i:
                for c in range(TPI):
                    n = i * TPI + c
                    pool.wait_ge(s_rows, n + 1 + CREDIT)
                    pool.wait_ge(s_meta, n + 1)
                    g.tensor_tensor(ids[:, :, :], ids[:, :, :], chunk_step[:, :, :], ALU.add).then_inc(s_ids, 1)
                    for k in range(TOPK):
                        for gr in range(NG):
                            g.indirect_dma_start(
                                out=slots[:, :],
                                out_offset=bass.IndirectOffsetOnAxis(
                                    ap=dest[c][:, k * NG + gr:k * NG + gr + 1], axis=0),
                                in_=rows[c][:, k, gr, :], in_offset=None).then_inc(s_scat[c], 16)
            with pool.Fori(0, NT // FPI) as i:
                for u in range(FPI):
                    t = i * FPI + u
                    pool.wait_ge(s_y, t + 1 + CREDIT)
                    pool.wait_ge(s_ret, t + 1 + CREDIT)
                    pool.wait_ge(s_carrier, t + CREDIT)
                    g.tensor_tensor(carrier[:, :], zero_c[0:1, :], zero_c[0:1, :], ALU.add).then_inc(s_carrier, 1)
                    g.indirect_dma_start(
                        out=y_rows[:, :],
                        out_offset=bass.IndirectOffsetOnAxis(ap=ret[u][:, 0:1], axis=0),
                        in_=y_sb[u][:, :], in_offset=None,
                        bounds_check=YROWS - 1, oob_is_err=False).then_inc(s_ysc[u], 16)

        @block.scalar
        def _(act):
            a = nc.scalar
            for free in (s_km, s_rows, s_gx):
                act.sem_inc(free, CREDIT)
            act.dma_start(w1_sb[:, :].rearrange("d (e h) -> d e h", e=E),
                          w1.rearrange("e d h -> d e h")).then_inc(s_w1, 16)
            act.dma_start(w2_sb[:, :].rearrange("p (e f d) -> p e f d", e=E, f=NHALF),
                          w2.rearrange("e (f p) d -> p e f d", f=NHALF)).then_inc(s_w2, 16)
            act.preload_act_table_set("natural_log_exp_and_others")
            act.wait_ge(s_cst, NCST)
            act.wait_ge(s_wtp, 1)
            a.activation(wT[:, :, :], bank(1).rearrange("p (a c) -> p a c", a=4), ACT.Copy).then_inc(s_wt, 1)
            act.wait_ge(s_wtp, 2)
            a.activation(wgc[:, :], bank(0, E), ACT.Copy).then_inc(s_wt, 1)

            def norm_q_k_v(n, c):
                act.wait_ge(s_km, n + CREDIT)
                act.wait_ge(s_xc, n + 1)
                a.activation(sq[c][:, :], bank(XC_K, CT), ACT.Square).then_inc(s_sq, 1)

            def channel_rstd(n):
                act.wait_ge(s_var, n + 1)
                act.wait_ge(s_xn, n + CREDIT)
                a.activation(lnv[:, :], bank(VAR_Q, CT), ACT.Ln, bias=eps_c[:, 0:1]).then_inc(s_lnv, 1)
                act.wait_ge(s_lnv, n + 1)
                a.activation(rstd[:, :], lnv[:, :], ACT.Exp, scale=-0.5).then_inc(s_rs, 1)

            def token_rstd(n):
                act.wait_ge(s_bmv, n + 1)
                a.activation(lnv2[:, :], bmv[:, :, 1], ACT.Ln, bias=eps_t[0:GT, 0:1]).then_inc(s_lnv2, 1)
                act.wait_ge(s_lnv2, n + 1)
                a.activation(rstd2[:, :], lnv2[:, :], ACT.Exp, scale=-0.5).then_inc(s_rs2, 1)

            def masked_keys(n, c):
                act.wait_ge(s_kp, n + 1)
                for hq in range(HQ):
                    last = a.activation(km[c][:, hq, :], bank(XC_K, CT), ACT.Identity,
                                        bias=zero_c[:, 0:1], scale=kmask[:, hq:hq + 1])
                last.then_inc(s_km, 1)

            def values(n, c):
                act.wait_ge(s_vp, n + 1)
                a.activation(vs[c][:, :], bank(V_B, NG * C), ACT.Copy).then_inc(s_vs, 1)

            def exps(n, c):
                act.wait_ge(s_sub, n + 1 + CREDIT)
                a.activation(ex[c][:, :, 0:W], es[c][:, :, :], ACT.Exp).then_inc(s_e, 1)

            def first_heads(n, c):
                act.wait_ge(s_av, n + 1)
                a.activation(av0[:, :].rearrange("p (r n) -> p r n", r=RG), av_view[:, :, 0, :], ACT.Identity,
                             bias=zero_c[:, 0:1], scale=pmask[:, 0:1]).then_inc(s_av0, 1)

            def keep_t(n, c):
                act.wait_ge(s_t, n + 1 + CREDIT)
                a.activation(t_sb[:, bass.ds(n * CT, CT)], tc[c][:, :], ACT.Copy).then_inc(s_tcp, 1)

            def normed_rows(n, c):
                act.wait_ge(s_st, n + 1)
                act.wait_ge(s_free, n + 1)
                for k in range(TOPK):
                    for gr in range(NG):
                        last = a.activation(rows[c][:, k, gr, 0:C],
                                            ps[0:GT, TR_B * 512 + gr * P:TR_B * 512 + gr * P + C], ACT.Identity,
                                            bias=nmr[:, gr:gr + 1], scale=rstd2[:, gr:gr + 1])
                last.then_inc(s_rows, 1)

            def gate_exps(n, c):
                act.wait_ge(s_m0, n + 1)
                for gr in range(NG):
                    a.activation(junk[:, gr, :], lg[:, gr, :], ACT.Exp, bias=nm0[:, gr:gr + 1],
                                 accum_out=esum[:, gr:gr + 1])
                a.activation(e2[:, :], dm[:, :], ACT.Exp).then_inc(s_gx, 1)

            def chunk(n, c, more):
                o = 1 - c
                if more:
                    norm_q_k_v(n + 1, o)
                    channel_rstd(n + 1)
                first_heads(n, c)
                if more:
                    masked_keys(n + 1, o)
                keep_t(n, c)
                token_rstd(n)
                if more:
                    values(n + 1, o)
                normed_rows(n, c)
                if more:
                    exps(n + 1, o)
                gate_exps(n, c)

            act.wait_ge(s_cstv, 2)
            norm_q_k_v(0, 0)
            channel_rstd(0)
            masked_keys(0, 0)
            values(0, 0)
            exps(0, 0)
            with act.Fori(0, NCH // TPI - 1) as i:
                for c in range(TPI):
                    chunk(i * TPI + c, c, True)
            for c in range(TPI):
                chunk(NCH - TPI + c, c, c + 1 < TPI)

            def take_xT(t, q):
                act.wait_ge(s_trx, t + 1 + CREDIT)
                if not isinstance(t, int) or t >= 2:
                    act.wait_ge(s_h, t - 1)
                a.activation(xT[q][:, :], bank(q, TS), ACT.Copy).then_inc(s_xT, 1)

            def gelu(t, q):
                act.wait_ge(s_h, t + 1)
                if not isinstance(t, int) or t >= 2:
                    act.wait_ge(s_th, t - 1 + CREDIT)
                a.activation(h_sb[q][:, :], bank(2 + q, HID), ACT.Gelu).then_inc(s_g, 1)

            take_xT(0, 0)
            take_xT(1, 1)
            gelu(0, 0)
            with act.Fori(0, NT // FPI) as i:
                for u in range(FPI):
                    t = i * FPI + u
                    take_xT(t + 2, u % 2)
                    act.wait_ge(s_h, t + 2)
                    act.wait_ge(s_th, t + CREDIT)
                    a.activation(h_sb[(u + 1) % 2][:, :], bank(2 + (u + 1) % 2, HID), ACT.Gelu).then_inc(s_g, 1)

        @block.vector
        def _(dve):
            v = nc.vector
            for free in (s_xn, s_q, s_o, s_sub, s_t, s_pb, s_macc, s_hT, s_y, s_ret):
                dve.sem_inc(free, CREDIT)
            v.memset(zero_c[:, :], 0.0)
            v.memset(eps_c[:, :], EPS_C)
            v.memset(eps_t[:, :], EPS_T)
            v.memset(pad_rows[:, :], 0.0).then_inc(s_cstv, 1)
            dve.wait_ge(s_cstv, 1)
            v.memset(pad_rows[:, ID:ID + 1].bitcast(I32), SKIP)
            v.memset(avg[:, :], 1.0 / C)
            v.memset(ones[:, :], 1.0)
            v.memset(one_e[:, :], 1.0)
            v.memset(macc[:, :], 0.0)
            v.memset(maccb[:, :], 0.0)
            v.memset(past[:, :, 0:1], 1.0)
            for c in range(2):
                v.memset(xn[c][:, :], 0.0)
                v.memset(qs[c][:, :], 0.0)
                v.memset(ex[c][:, :, :], 0.0)
                v.memset(rows[c][:, :, :, C:], 0.0)
            dve.wait_ge(s_cst, NCST)
            for f in range(HF):
                v.tensor_scalar(hscale[:, f, :], hmask[:, f * HQ:(f + 1) * HQ], SCALE, None,
                                ALU.mult).then_inc(s_masks, 1)
            v.tensor_reduce(pmask[:, :], hmask[:, :].rearrange("c (p a) -> c a p", a=2), AX.X,
                            ALU.add).then_inc(s_masks, 1)
            dve.wait_ge(s_masks, 3)
            v.tensor_tensor(kmask[:, :], hscale[:, 0, :], hscale[:, 1, :], ALU.add)
            v.tensor_scalar(cmat[:, :], ident[:, :], -1.0 / C, None, ALU.add).then_inc(s_cstv, 1)
            def layer_norm(n, c):
                dve.wait_ge(s_rs, n + 1)
                v.tensor_tensor(xn[c][:, :].rearrange("p (a w) -> p a w", w=WP)[:, :, 0:W],
                                bank(XC_K, CT).rearrange("p (a w) -> p a w", w=W),
                                rstd[:, :].rearrange("p (a w) -> p a w", w=W), ALU.mult).then_inc(s_xn, 1)

            def queries(n, c):
                dve.wait_ge(s_qp, n + 1)
                v.tensor_copy(qs[c][:, :].rearrange("p (a w) -> p a w", w=WP)[:, :, 0:W],
                              bank(VAR_Q, CT).rearrange("p (a w) -> p a w", w=W)).then_inc(s_q, 1)

            NS = HF * NG * HQ

            def row_max(n, c):
                dve.wait_ge(s_s, n + 1)
                v.tensor_reduce(mx[:, :].rearrange("p (f a) -> p f a", f=HF), s_view, AX.X,
                                ALU.max).then_inc(s_mx, 1)
                dve.wait_ge(s_mx, n + 1)
                v.tensor_tensor(es[c][:, :, :].rearrange("p (f a) j -> p f a j", f=HF), s_view,
                                mx[:, :].rearrange("p (f a) -> p f a", f=HF).unsqueeze(3)
                                .broadcast_to([P, HF, NG * HQ, W]), ALU.subtract).then_inc(s_sub, 1)

            def row_sum(n, c):
                dve.wait_ge(s_e, n + 1)
                v.tensor_reduce(den[:, :], ex[c][:, :, 0:W], AX.X, ALU.add).then_inc(s_den, 1)

            def normalise(n, c):
                dve.wait_ge(s_den, n + 1)
                v.reciprocal(rden[:, :], den[:, :]).then_inc(s_rden, 1)

            def spread(n, c):
                dve.wait_ge(s_rden, n + 1)
                v.tensor_tensor(ex[c][:, :, 0:W], ex[c][:, :, 0:W],
                                rden[:, :].unsqueeze(2).broadcast_to([P, NS, W]), ALU.mult).then_inc(s_nrm, 1)
                dve.wait_ge(s_nrm, n + 1)
                v.transpose(exT[c][:, :, :].rearrange("p a w -> p (a w)"),
                            ex[c][:, :, :].rearrange("p a w -> p (a w)")).then_inc(s_et, 1)

            def attn_out(n, c):
                dve.wait_ge(s_av0, n + 1)
                v.scalar_tensor_tensor(o_sb[c][:, :].rearrange("p (r n) -> p r n", r=RG), av_view[:, :, 1, :],
                                       pmask[:, 1:2], av0[:, :].rearrange("p (r n) -> p r n", r=RG),
                                       ALU.mult, ALU.add).then_inc(s_o, 1)

            def residual(n, c):
                dve.wait_ge(s_pj, n + 1)
                v.scalar_tensor_tensor(tc[c][:, :], bank(PJ_B, CT), bo[:, 0:1], x_sb[:, bass.ds(n * CT, CT)],
                                       ALU.add, ALU.add).then_inc(s_t, 1)

            def token_stats(n, c):
                dve.wait_ge(s_tr, n + 1)
                for gr in range(NG):
                    last = v.bn_stats(bst[:, gr, :], ps[0:GT, TR_B * 512 + gr * P:TR_B * 512 + gr * P + C])
                last.then_inc(s_bst, 1)
                dve.wait_ge(s_win, 64)
                dve.wait_ge(s_bst, n + 1)
                dve.wait_ge(s_rows, n + CREDIT)
                for gr in range(NG):
                    last = v.bn_aggr(bmv[:, gr, :], bst[:, gr, :])
                last.then_inc(s_bmv, 1)
                dve.wait_ge(s_bmv, n + 1)
                dve.wait_ge(s_rs2, n + 1)
                v.scalar_tensor_tensor(nmr[:, :], bmv[:, :, 0], -1.0, rstd2[:, :], ALU.mult,
                                       ALU.mult).then_inc(s_st, 1)

            def top2(n, c):
                dve.wait_ge(s_lg, n + 1)
                dve.wait_ge(s_gx, n + CREDIT)
                v.tensor_tensor(lg[:, :, :], LG.rearrange("p (g e) -> p g e", g=NG),
                                rstd2[:, :].unsqueeze(2).broadcast_to([GT, NG, E]), ALU.mult).then_inc(s_lgs, 1)
                dve.wait_ge(s_win, 64)
                dve.wait_ge(s_lgs, n + 1)
                for gr in range(NG):
                    last = v.max(m8[:, gr, :], lg[:, gr, :])
                last.then_inc(s_m8, 1)
                dve.wait_ge(s_win, 64)
                dve.wait_ge(s_m8, n + 1)
                for gr in range(NG):
                    last = v.max_index(i8[:, gr, :], m8[:, gr, :], lg[:, gr, :])
                last.then_inc(s_i8, 1)
                v.tensor_tensor(dm[:, :], m8[:, :, 1], m8[:, :, 0], ALU.subtract)
                v.tensor_scalar(nm0[:, :], m8[:, :, 0], -1.0, None, ALU.mult).then_inc(s_m0, 1)
                dve.wait_ge(s_i8, n + 1)
                v.tensor_copy(idx[:, :, :], i8[:, :, 0:TOPK].rearrange("p g k -> p k g")).then_inc(s_idx, 1)
                dve.wait_ge(s_idx, n + 1)
                v.tensor_tensor(oh[:, :, :].rearrange("p k (g e) -> p (k g) e", e=E),
                                iota_e[0:GT, :].unsqueeze(1).broadcast_to([GT, TOPK * NG, E]),
                                idx[:, :, :].rearrange("p k g -> p (k g)").unsqueeze(2)
                                .broadcast_to([GT, TOPK * NG, E]), ALU.is_equal).then_inc(s_oh, 1)
                dve.wait_ge(s_oh, n + 1)
                v.tensor_tensor(mt[:, :, :].rearrange("p g e -> p (g e)"), oh[:, 0, :], oh[:, 1, :],
                                ALU.add).then_inc(s_mt, 1)

            def slot_rows(n, c):
                dve.wait_ge(s_mt, n + 1)
                v.tensor_reduce(msum[:, :], mt[:, :, :].rearrange("p g e -> p e g"), AX.X,
                                ALU.add).then_inc(s_ms, 1)
                dve.wait_ge(s_pos, n + 1)
                v.tensor_tensor(posb[:, :].rearrange("p (g e) -> p g e", g=NG),
                                POS.rearrange("p (g e) -> p g e", g=NG),
                                ebase[0:GT, :].unsqueeze(1).broadcast_to([GT, NG, E]), ALU.add).then_inc(s_pb, 1)
                dve.wait_ge(s_ms, n + 1)
                v.tensor_tensor(macc[:, :], macc[:, :], msum[:, :], ALU.add).then_inc(s_ma, 1)
                dve.wait_ge(s_pb, n + 1 + CREDIT)
                v.tensor_tensor(prod[:, :, :], oh[:, :, :], posb[:, :].unsqueeze(1)
                                .broadcast_to([GT, TOPK, NG * E]), ALU.mult).then_inc(s_pr, 1)
                dve.wait_ge(s_ma, n + 1)
                v.tensor_copy(maccb[:, :], macc[:, :]).then_inc(s_macc, 1)
                dve.wait_ge(s_pr, n + 1)
                v.tensor_reduce(destf[:, :], prod[:, :, :].rearrange("p k (g e) -> p (k g) e", e=E), AX.X,
                                ALU.add).then_inc(s_df, 1)
                dve.wait_ge(s_gx, n + 1 + CREDIT)
                v.reciprocal(rg[:, :], esum[:, :]).then_inc(s_rg, 1)
                dve.wait_ge(s_free, n + 1)
                dve.wait_ge(s_df, n + 1)
                v.tensor_copy(dest[c][:, :], destf[:, :])
                dve.wait_ge(s_ids, n + CREDIT)
                v.tensor_copy(rows[c][:, :, :, ID].bitcast(U32), ids[:, :, :])
                dve.wait_ge(s_rg, n + 1)
                v.tensor_copy(rows[c][:, 0, :, GATE], rg[:, :])
                v.tensor_tensor(rows[c][:, 1, :, GATE], rg[:, :], e2[:, :], ALU.mult).then_inc(s_meta, 1)

            def chunk(n, c, more):
                o = 1 - c
                if more:
                    layer_norm(n + 1, o)
                attn_out(n, c)
                if more:
                    queries(n + 1, o)
                residual(n, c)
                token_stats(n, c)
                if more:
                    row_max(n + 1, o)
                top2(n, c)
                if more:
                    row_sum(n + 1, o)
                    normalise(n + 1, o)
                    spread(n + 1, o)
                slot_rows(n, c)

            dve.wait_ge(s_win, 64)
            layer_norm(0, 0)
            queries(0, 0)
            row_max(0, 0)
            row_sum(0, 0)
            normalise(0, 0)
            spread(0, 0)
            with dve.Fori(0, NCH // TPI - 1) as i:
                for c in range(TPI):
                    chunk(i * TPI + c, c, True)
            for c in range(TPI):
                chunk(NCH - TPI + c, c, c + 1 < TPI)

            step = [0]

            def then(ins):
                step[0] += 1
                ins.then_inc(s_v, 1)
                dve.wait_ge(s_v, step[0])

            dve.wait_ge(s_cnt, 1)
            then(v.tensor_copy(cnt[:, :], CNT))
            then(v.tensor_scalar(nt_i[:, :], cnt[:, :], float(TS - 1), None, ALU.add))
            then(v.tensor_scalar(nt_i[:, :], nt_i[:, :], TS.bit_length() - 1, None, ALU.logical_shift_right))
            then(v.tensor_copy(nt_f[:, :], nt_i[:, :]))
            then(v.tensor_tensor_scan(ct_f[:, :], one_e[:, :], nt_f[:, :], 0.0, ALU.mult, ALU.add))
            shape = [P, NTAB, E]
            then(v.tensor_tensor(past[:, :, 1:E + 1], iota_t[:, :].unsqueeze(2).broadcast_to(shape),
                                 ct_f[:, :].unsqueeze(1).broadcast_to(shape), ALU.is_ge))
            then(v.tensor_reduce(e_t[:, :], past[:, :, 1:E + 1], AX.X, ALU.add))
            then(v.tensor_tensor(tw[:, :, :], past[:, :, 1:E + 1], nt_f[:, :].unsqueeze(1).broadcast_to(shape),
                                 ALU.mult))
            then(v.tensor_reduce(first[:, :], tw[:, :, :], AX.X, ALU.add))
            then(v.tensor_tensor(tw[:, :, :], past[:, :, 0:E], past[:, :, 1:E + 1], ALU.subtract))
            then(v.tensor_tensor(tw[:, :, :], tw[:, :, :], cnt[:, :].unsqueeze(1).broadcast_to(shape), ALU.mult))
            then(v.tensor_reduce(c_t[:, :], tw[:, :, :], AX.X, ALU.add))
            then(v.tensor_tensor(j128[:, :], iota_t[:, :], first[:, :], ALU.subtract))
            then(v.tensor_scalar(j128[:, :], j128[:, :], float(TS), None, ALU.mult))
            then(v.scalar_tensor_tensor(start[:, :], c_t[:, :], -float(TS), j128[:, :], ALU.add, ALU.min))
            then(v.tensor_scalar(start[:, :], start[:, :], 0.0, None, ALU.max))
            then(v.tensor_scalar(skip[:, :], e_t[:, :], float(E), float(TS), ALU.is_equal, ALU.mult))
            then(v.tensor_tensor(skip[:, :], skip[:, :], j128[:, :], ALU.add))
            then(v.tensor_tensor(skip[:, :], skip[:, :], start[:, :], ALU.subtract))
            then(v.tensor_scalar(skip[:, :], skip[:, :], iota_p[:, 0:1], float(SKIP), ALU.is_gt, ALU.mult))
            then(v.tensor_scalar(e_c[:, :], e_t[:, :], float(E - 1), None, ALU.min))
            v.tensor_scalar(woff[:, :], e_c[:, :], float(HID), None, ALU.mult)
            v.scalar_tensor_tensor(rowoff[:, :], e_c[:, :], float(CAP), start[:, :], ALU.mult,
                                   ALU.add).then_inc(s_tab, 1)

            def tile(t, u, scattered):
                dve.wait_ge(s_ld[u], scattered + 16)
                if not isinstance(scattered, int):
                    dve.wait_ge(s_ysc[u], scattered)
                v.tensor_tensor(ret[u][:, :], xs[u][:, ID:ID + 1].bitcast(U32), skip[:, bass.ds(t, 1)],
                                ALU.add).then_inc(s_ret, 1)
                dve.wait_ge(s_th, t + 1 + CREDIT)
                v.tensor_copy(hT[u % 2][:, :], bank(4 + u % 2, HID)).then_inc(s_hT, 1)
                dve.wait_ge(s_yp, t + 1)
                v.tensor_scalar(y_sb[u][:, :], bank(6 + u % 2, C), xs[u][:, GATE:GATE + 1], None,
                                ALU.mult).then_inc(s_y, 1)

            for u in range(FPI):
                tile(u, u, 0)
            with dve.Fori(1, NT // FPI) as i:
                for u in range(FPI):
                    tile(i * FPI + u, u, i * 16)

            for b, (n0, n1) in enumerate(YB):
                dve.wait_ge(s_yk[b], 16 * TOPK)
                v.tensor_tensor(ysum[:, n0 * C:n1 * C], yk[:, 0, n0 * C:n1 * C], yk[:, 1, n0 * C:n1 * C],
                                ALU.add).then_inc(s_ys, 1)
            for b, (n0, n1) in enumerate(YB):
                dve.wait_ge(s_yt, b + 1)
                v.tensor_tensor(fin[:, n0 * P:n1 * P], ps[:, n0 * P:n1 * P], t_sb[:, n0 * P:n1 * P],
                                ALU.add).then_inc(s_fin, 1)

        @block.tensor
        def _(pe):
            mm = nc.tensor.matmul
            for free in (s_th, s_trx):
                pe.sem_inc(free, CREDIT)
            pe.wait_ge(s_cst, NCST)
            pe.wait_ge(s_win, 64)
            for k in range(3):
                nc.tensor.transpose(ps[:, 512 + k * C:512 + (k + 1) * C], wqkv_sb[:, k, :], ident[:, :])
            nc.tensor.transpose(ps[:, 512 + 3 * C:512 + 4 * C], wout_sb[:, :], ident[:, :]).then_inc(s_wtp, 1)
            pe.wait_ge(s_cstv, 2)
            mm(bank(0, E), cmat[:, :], wg[:, :], start=True, stop=True).then_inc(s_wtp, 1)
            pe.wait_ge(s_wt, 2)
            pe.wait_ge(s_xin[0], 16)

            def centre(n):
                pe.wait_ge(s_km, n + CREDIT)
                mm(bank(XC_K, CT), cmat[:, :], x_sb[:, bass.ds(n * CT, CT)], start=True,
                   stop=True).then_inc(s_xc, 1)

            def variance(n, c):
                pe.wait_ge(s_sq, n + 1)
                pe.wait_ge(s_q, n + CREDIT)
                mm(bank(VAR_Q, CT), avg[:, :], sq[c][:, :], start=True, stop=True).then_inc(s_var, 1)

            def project(n, c):
                pe.wait_ge(s_xn, n + 1 + CREDIT)
                xr = xn[c][:, :].rearrange("p (a w) -> p a w", w=WP)[:, :, 0:W]
                mm(bank(VAR_Q, CT), wT[:, 0, :], xr, start=True, stop=True).then_inc(s_qp, 1)
                mm(bank(XC_K, CT), wT[:, 1, :], xr, start=True, stop=True).then_inc(s_kp, 1)

            def value_rows(n, c):
                pe.wait_ge(s_o, n + CREDIT)
                for gr in range(NG):
                    last = mm(ps[:, V_B * 512 + gr * C:V_B * 512 + (gr + 1) * C], xn[c][:, gr * P:(gr + 1) * P],
                              wT[:, 2, :], start=True, stop=True)
                last.then_inc(s_vp, 1)

            def scores(n, c):
                pe.wait_ge(s_wt, 2)
                pe.wait_ge(s_q, n + 1 + CREDIT)
                pe.wait_ge(s_km, n + 1 + CREDIT)
                pe.wait_ge(s_sub, n + CREDIT)
                for gr in range(NG):
                    for r in range(RG):
                        row = gr * RG + r
                        for f in range(HF):
                            col = (S0 + f) * 512 + gr * HQ * W
                            last = mm(ps[r * 32:(r + 1) * 32, col:col + HQ * W],
                                      qs[c][f * 64:(f + 1) * 64, row * WP:(row + 1) * WP],
                                      km[c][f * 64:(f + 1) * 64, :, row * W:(row + 1) * W],
                                      start=True, stop=True)
                last.then_inc(s_s, 1)

            def attend(n, c):
                pe.wait_ge(s_wt, 2)
                pe.wait_ge(s_et, n + 1)
                pe.wait_ge(s_vs, n + 1)
                pe.wait_ge(s_t, n + CREDIT)
                pe.wait_ge(s_rows, n + CREDIT)
                pe.wait_ge(s_pb, n + CREDIT)
                for gr in range(NG):
                    for p in range(NP):
                        for r in range(RG):
                            a0 = (2 * p // HQ) * NG * HQ + gr * HQ + 2 * p % HQ
                            out_ap = av_view[p * 32:(p + 1) * 32, r, :, gr * W:(gr + 1) * W]
                            last = mm(out_ap,
                                      vs[c][r * 32:(r + 1) * 32, gr * C + p * 32:gr * C + (p + 1) * 32],
                                      exT[c][r * 32:(r + 1) * 32, a0:a0 + 2, 0:W], start=True, stop=True)
                last.then_inc(s_av, 1)

            def out_proj(n, c):
                pe.wait_ge(s_o, n + 1 + CREDIT)
                mm(bank(PJ_B, CT), wT[:, 3, :],
                   o_sb[c][:, :].rearrange("p (r g i) -> p g r i", r=RG, g=NG), start=True, stop=True).then_inc(s_pj, 1)

            def token_major(n, c):
                pe.wait_ge(s_t, n + 1 + CREDIT)
                for gr in range(NG):
                    last = nc.tensor.transpose(ps[0:GT, TR_B * 512 + gr * P:TR_B * 512 + gr * P + C],
                                               tc[c][:, gr * GT:(gr + 1) * GT], ident[:, :])
                last.then_inc(s_tr, 1)
                for gr in range(NG):
                    last = mm(LG[:, gr * E:(gr + 1) * E], tc[c][:, gr * GT:(gr + 1) * GT], wgc[:, :],
                              start=True, stop=True)
                last.then_inc(s_lg, 1)

            def places(n):
                pe.wait_ge(s_macc, n + CREDIT)
                pe.wait_ge(s_mt, n + 1)
                for gr in range(NG):
                    col = POS[:, gr * E:(gr + 1) * E]
                    mm(col, ones[:, 0:GT], maccb[:, :], start=True, stop=False)
                    for before in range(gr):
                        mm(col, ones[:, 0:GT], mt[:, before, :], start=False, stop=False)
                    last = mm(col, tri[:, :], mt[:, gr, :], start=False, stop=True)
                last.then_inc(s_pos, 1)

            def chunk(n, c, more):
                o = 1 - c
                if more:
                    centre(n + 1)
                attend(n, c)
                if more:
                    variance(n + 1, o)
                    project(n + 1, o)
                out_proj(n, c)
                if more:
                    value_rows(n + 1, o)
                token_major(n, c)
                if more:
                    scores(n + 1, o)
                places(n)

            centre(0)
            variance(0, 0)
            project(0, 0)
            value_rows(0, 0)
            scores(0, 0)
            pe.wait_ge(s_xin[1], 16)
            with pe.Fori(0, NCH // TPI - 1) as i:
                for c in range(TPI):
                    chunk(i * TPI + c, c, True)
            for c in range(TPI):
                chunk(NCH - TPI + c, c, c + 1 < TPI)
            pe.wait_ge(s_macc, NCH + CREDIT)
            mm(CNT, ones[:, :], maccb[:, :], start=True, stop=True).then_inc(s_cnt, 1)

            pe.wait_ge(s_tab, 1)
            pe.wait_ge(s_w1, 16)
            pe.wait_ge(s_w2, 16)

            def rows_T(u, q):
                nc.tensor.transpose(bank(q, TS), xs[u][:, 0:C], ident[:, :]).then_inc(s_trx, 1)

            pe.wait_ge(s_ld[0], 16)
            rows_T(0, 0)
            pe.wait_ge(s_ld[1], 16)
            rows_T(1, 1)
            wo = pe.value_load(woff[0:1, 0:1], min_val=0, max_val=(E - 1) * HID)
            pe.wait_ge(s_xT, 1)
            mm(bank(2, HID), xT[0][:, :], w1_sb[:, bass.ds(wo, HID)], start=True, stop=True).then_inc(s_h, 1)
            with pe.Fori(0, NT // FPI) as i:
                for u in range(FPI):
                    t = i * FPI + u
                    q, o = u % 2, (u + 1) % 2
                    w_now = pe.value_load(woff[0:1, bass.ds(t, 1)], min_val=0, max_val=(E - 1) * HID)
                    w_next = pe.value_load(woff[0:1, bass.ds(t + 1, 1)], min_val=0, max_val=(E - 1) * HID)
                    pe.wait_ge(s_ld[(u + 2) % AHEAD], i * 16 + 16 * (1 + (u + 2) // AHEAD))
                    pe.wait_ge(s_xT, t + 1)
                    rows_T((u + 2) % AHEAD, q)
                    pe.wait_ge(s_g, t + 1)
                    pe.wait_ge(s_hT, t + CREDIT)
                    for f in range(NHALF):
                        last = nc.tensor.transpose(ps[:, (4 + q) * 512 + f * P:(4 + q) * 512 + (f + 1) * P],
                                                   h_sb[q][:, f * P:(f + 1) * P], ident[:, :])
                    last.then_inc(s_th, 1)
                    pe.wait_ge(s_xT, t + 2)
                    mm(bank(2 + o, HID), xT[o][:, :], w1_sb[:, bass.ds(w_next, HID)], start=True,
                       stop=True).then_inc(s_h, 1)
                    pe.wait_ge(s_hT, t + 1 + CREDIT)
                    pe.wait_ge(s_y, t + CREDIT)
                    for f in range(NHALF):
                        last = mm(bank(6 + q, C), hT[q][:, f * P:(f + 1) * P],
                                  w2_sb[:, bass.ds(w_now + f * C, C)], start=(f == 0), stop=(f == NHALF - 1))
                    last.then_inc(s_yp, 1)

            pe.wait_ge(s_y, NT + CREDIT)
            pe.wait_ge(s_g, NT + 1)
            pe.wait_ge(s_xT, NT + 2)
            for b, (n0, n1) in enumerate(YB):
                pe.wait_ge(s_ys, b + 1)
                for m in range(n0, n1):
                    last = nc.tensor.transpose(ps[:, m * P:(m + 1) * P], ysum[:, m * C:(m + 1) * C], ident[:, :])
                last.then_inc(s_yt, 1)


_INS = ["x", "L0_conv_w_qkv", "L0_conv_w_out", "L0_conv_b_out", "L0_ffn_W_gate", "L0_ffn_W1", "L0_ffn_W2"]


def kernel(**inputs):
    import concourse.bacc as bacc
    from concourse.bass_utils import run_bass_kernel_spmd

    nc = bacc.Bacc("TRN2", target_bir_lowering=False, num_devices=1)
    arrays, args = {}, []
    for name in _INS:
        a = np.ascontiguousarray(inputs[name])
        arrays[f"in_{name}"] = a
        args.append(nc.dram_tensor(f"in_{name}", a.shape, mybir.dt.from_np(a.dtype), kind="ExternalInput").ap())
    out = nc.dram_tensor("out_x", (B, C, H, W), F32, kind="ExternalOutput").ap()
    build(nc, *args, out)
    r = run_bass_kernel_spmd(nc, [arrays], core_ids=[0])
    return r.results[0]["out_x"]
```

```python
from contextlib import ExitStack

import numpy as np
import concourse.bass as bass
from concourse import mybir

F32 = mybir.dt.float32
BF16 = mybir.dt.bfloat16
I32 = mybir.dt.int32
U32 = mybir.dt.uint32
ALU = mybir.AluOpType
ACT = mybir.ActivationFunctionType
AX = mybir.AxisListType

P = 128
B, C, H, W = 4, 128, 24, 24
HEADS = 8
HD = C // HEADS
SCALE = HD ** -0.5
E = 16
HID = 256
NHALF = HID // P
EPS_C = 1e-6
EPS_T = 1e-5
TOK = B * H * W

RG = 4
WP = 32
GT = RG * W
NG = 3
CT = NG * GT
CR = NG * RG
NCH = TOK // CT
HF = 2
HQ = HEADS // HF
NP = HEADS // 2
TOPK = 2

TS = 128
CAP = TOK + TS
RW = C + 4
ID, GATE = C, C + 1
NT = (TOPK * TOK + E * (TS - 1)) // TS + 1
XB = 8
WB = 4
HEAD = NT % XB
LOOPS = NT // XB - 1
YROWS = TOPK * TOK
IN_RANGE = "clamped where the tile table is worked out"
SKIP = 8192


def build(nc, x, w_qkv, w_out, b_out, w_gate, w1, w2, out):
    x_v = x.rearrange("b c h w -> c b (h w)")
    out_v = out.rearrange("b c h w -> c b (h w)")
    slots = nc.dram_tensor("slots", (E * CAP, RW), F32, kind="Internal").ap()
    y_rows = nc.dram_tensor("y_rows", (YROWS, C), F32, kind="Internal").ap()

    ctx = ExitStack()
    with ctx:
        def sb(name, shape, dt=F32):
            return ctx.enter_context(nc.sbuf_tensor(name, shape, dt))

        def sem(name):
            return ctx.enter_context(nc.semaphore(name))

        x_sb = sb("x_sb", [P, TOK])
        t_sb = sb("t_sb", [P, TOK])
        wqkv_sb = sb("wqkv_sb", [P, 3, C])
        wout_sb = sb("wout_sb", [P, C])
        wT = sb("wT", [P, 4, C])
        bo = sb("bo", [P, 1])
        wg = sb("wg", [P, E])
        wgc = sb("wgc", [P, E])
        w_sb = sb("w_sb", [P, E, HID + NHALF * C])
        ident = sb("ident", [P, P])
        cmat = sb("cmat", [P, P])
        avg = sb("avg", [P, P])
        tri = sb("tri", [GT, GT], BF16)
        ones = sb("ones", [GT, P], BF16)
        hmask = sb("hmask", [P, HEADS])
        kmask = sb("kmask", [P, HQ])
        hscale = sb("hscale", [P, HF, HQ])
        pmask = sb("pmask", [P, 2])
        iota_e = sb("iota_e", [P, E])
        ebase = sb("ebase", [P, E])
        ids = sb("ids", [GT, TOPK, NG])
        chunk_step = sb("chunk_step", [GT, TOPK, NG])
        zero_c = sb("zero_c", [P, 1])
        eps_c = sb("eps_c", [P, 1])
        eps_t = sb("eps_t", [P, 1])
        lnv = sb("lnv", [P, CT])
        lnv2 = sb("lnv2", [GT, NG])
        pad_rows = sb("pad_rows", [P, RW])
        padid = sb("padid", [P, 1])

        sq = [sb(f"sq{i}", [P, CT]) for i in range(2)]
        rstd = sb("rstd", [P, CT])
        xn = [sb(f"xn{i}", [P, CR * WP]) for i in range(2)]
        qs = [sb(f"qs{i}", [P, CR * WP]) for i in range(2)]
        km = [sb(f"km{i}", [P, HQ, CT]) for i in range(2)]
        vs = [sb(f"vs{i}", [P, NG * C]) for i in range(2)]
        mx = sb("mx", [P, HF * NG * HQ])
        den = sb("den", [P, HF * NG * HQ])
        rden = sb("rden", [P, HF * NG * HQ])
        es = [sb(f"es{i}", [P, HF * NG * HQ, W]) for i in range(2)]
        ex = [sb(f"ex{i}", [P, HF * NG * HQ, WP]) for i in range(2)]
        exT = [sb(f"exT{i}", [P, HF * NG * HQ, WP]) for i in range(2)]
        av0 = sb("av0", [P, CT])
        o_sb = [sb(f"o_sb{i}", [P, CT]) for i in range(2)]
        tc = [sb(f"tc{i}", [P, CT]) for i in range(2)]
        bst = sb("bst", [GT, NG, 6])
        bmv = sb("bmv", [GT, NG, 2])
        rstd2 = sb("rstd2", [GT, NG])
        nmr = sb("nmr", [GT, NG])
        rows = [sb(f"rows{i}", [GT, TOPK, NG, RW]) for i in range(2)]
        lg = sb("lg", [GT, NG, E])
        m8 = sb("m8", [GT, NG, 8])
        i8 = sb("i8", [GT, NG, 8], U32)
        idx = sb("idx", [GT, TOPK, NG])
        nm0 = sb("nm0", [GT, NG])
        dm = sb("dm", [GT, NG])
        junk = sb("junk", [GT, NG, E])
        esum = sb("esum", [GT, NG])
        e2 = sb("e2", [GT, NG])
        oh = sb("oh", [GT, TOPK, NG * E])
        mt = sb("mt", [GT, NG, E], BF16)
        msum = sb("msum", [GT, E])
        macc = sb("macc", [GT, E])
        maccb = sb("maccb", [GT, E], BF16)
        posb = sb("posb", [GT, NG * E])
        prod = sb("prod", [GT, TOPK, NG * E])
        destf = sb("destf", [GT, TOPK * NG])
        dest = [sb(f"dest{i}", [GT, TOPK * NG], U32) for i in range(2)]
        rg = sb("rg", [GT, NG])

        iota_t = sb("iota_t", [P, NT])
        iota_p = sb("iota_p", [P, 1])
        cnt = sb("cnt", [P, E])
        nt_i = sb("nt_i", [P, E], I32)
        nt_f = sb("nt_f", [P, E])
        ct_f = sb("ct_f", [P, E])
        one_e = sb("one_e", [P, E])
        past = sb("past", [P, NT, E + 1])
        tw = sb("tw", [P, NT, E])
        first = sb("first", [P, NT])
        c_t = sb("c_t", [P, NT])
        e_t = sb("e_t", [P, NT])
        j128 = sb("j128", [P, NT])
        start = sb("start", [P, NT])
        skip = sb("skip", [P, NT])
        e_c = sb("e_c", [P, NT])
        rowoff = sb("rowoff", [P, NT], I32)
        woff = sb("woff", [P, NT], I32)

        we = [sb(f"we{i}", [P, HID + NHALF * C]) for i in range(WB)]
        xs = [sb(f"xs{i}", [P, RW]) for i in range(XB)]
        xT = [sb(f"xT{i}", [P, TS]) for i in range(2)]
        hT = [sb(f"hT{i}", [P, NHALF, TS]) for i in range(2)]
        y_sb = [sb(f"y_sb{i}", [P, C]) for i in range(XB)]
        ret = [sb(f"ret{i}", [P, 1], U32) for i in range(XB)]
        gate = [sb(f"gate{i}", [P, 1]) for i in range(XB)]

        NY = TOK // P
        FB = 4
        YB = [(m, min(m + FB, NY)) for m in range(0, NY, FB)]
        yk = sb("yk", [P, TOPK, NY * C])
        ysum = sb("ysum", [P, NY * C])
        fin = x_sb

        ps = ctx.enter_context(nc.psum_tensor("ps", [P, 8 * 512], F32))

        def bank(i, n=512, p=P):
            return ps[0:p, i * 512:i * 512 + n]

        XC_K, VAR_Q, S0, AV0, V_B, PJ_B, TR_B, RT_B = 0, 1, 2, 4, 4, 5, 6, 7
        LG = ps[0:GT, RT_B * 512:RT_B * 512 + NG * E]
        POS = ps[0:GT, RT_B * 512 + 64:RT_B * 512 + 64 + NG * E]
        CNT = ps[0:P, RT_B * 512 + 128:RT_B * 512 + 128 + E]
        s_view = ps[:, S0 * 512:(S0 + 2) * 512].rearrange("p (f n) -> p f n", f=HF)[:, :, 0:NG * HQ * W] \
            .rearrange("p f (a j) -> p f a j", j=W)
        av_view = ps[:, AV0 * 512:(AV0 + 4) * 512].rearrange("p (r n) -> p r n", r=RG)[:, :, 0:2 * NG * W] \
            .rearrange("p r (a n) -> p r a n", a=2)

        s_cst = sem("s_cst")
        s_cstv = sem("s_cstv")
        s_free = sem("s_free")
        s_carrier = sem("s_carrier")
        s_masks = sem("s_masks")
        s_xin = [sem(f"s_xin{i}") for i in range(2)]
        s_win = sem("s_win")
        s_wl = sem("s_wl")
        s_pre = sem("s_pre")
        s_wtp = sem("s_wtp")
        s_wt = sem("s_wt")
        s_v = sem("s_v")
        s_xc = sem("s_xc")
        s_sq = sem("s_sq")
        s_var = sem("s_var")
        s_xn = sem("s_xn")
        s_qp = sem("s_qp")
        s_kp = sem("s_kp")
        s_q = sem("s_q")
        s_km = sem("s_km")
        s_vp = sem("s_vp")
        s_vs = sem("s_vs")
        s_s = sem("s_s")
        s_sub = sem("s_sub")
        s_e = sem("s_e")
        s_et = sem("s_et")
        s_av = sem("s_av")
        s_av0 = sem("s_av0")
        s_o = sem("s_o")
        s_pj = sem("s_pj")
        s_t = sem("s_t")
        s_tcp = sem("s_tcp")
        s_tr = sem("s_tr")
        s_lg = sem("s_lg")
        s_st = sem("s_st")
        s_rows = sem("s_rows")
        s_m0 = sem("s_m0")
        s_mt = sem("s_mt")
        s_gx = sem("s_gx")
        s_pos = sem("s_pos")
        s_pb = sem("s_pb")
        s_macc = sem("s_macc")
        s_meta = sem("s_meta")
        s_scat = [sem(f"s_scat{i}") for i in range(2)]
        s_cnt = sem("s_cnt")
        s_tab = sem("s_tab")
        s_ld = [sem(f"s_ld{i}") for i in range(XB)]
        s_trx = sem("s_trx")
        s_xT = sem("s_xT")
        s_h = sem("s_h")
        s_g = sem("s_g")
        s_we = sem("s_we")
        s_yp = sem("s_yp")
        s_y = sem("s_y")
        s_ret = sem("s_ret")
        s_ysc = [sem(f"s_ysc{i}") for i in range(XB)]
        s_yk = [sem(f"s_yk{i}") for i in range(len(YB))]
        s_ys = sem("s_ys")
        s_yt = sem("s_yt")
        s_fin = sem("s_fin")
        s_out = sem("s_out")

        s_rs, s_mx, s_den, s_rden, s_nrm, s_bst, s_bmv, s_rs2, s_lgs, s_m8, s_i8, s_idx, s_oh, s_ms, s_ma, \
            s_pr, s_df, s_rg, s_ids, s_lnv, s_lnv2 = [sem(f"s_{k}") for k in (
                "rs", "mx", "den", "rden", "nrm", "bst", "bmv", "rs2", "lgs", "m8", "i8", "idx", "oh", "ms",
                "ma", "pr", "df", "rg", "ids", "lnv", "lnv2")]

        NCST = 12
        CREDIT = 1
        TPI = 2

        def tiles(eng, step, last=NT):
            for j in range(HEAD):
                step(0, j)
            with eng.Fori(0, LOOPS) as i:
                for j in range(HEAD, HEAD + XB):
                    step(i, j)
            for t in range(HEAD + LOOPS * XB, last):
                step(0, t)

        def used(i, j):
            return i * 16 + 16 * (j // XB + 1)


        block = ctx.enter_context(nc.Block())

        @block.sync
        def _(sp):
            sp.dma_start(wqkv_sb[:, :, :], w_qkv.rearrange("(a o) c -> o a c", a=3)).then_inc(s_win, 16)
            sp.dma_start(x_sb[:, 0:TOK // B], x_v[:, 0, :]).then_inc(s_xin[0], 16)
            sp.dma_start(wout_sb[:, :], w_out).then_inc(s_win, 16)
            sp.dma_start(bo[:, :], b_out.rearrange("(c a) -> c a", a=1)).then_inc(s_win, 16)
            sp.dma_start(wg[:, :], w_gate).then_inc(s_win, 16)
            sp.dma_start(x_sb[:, TOK // B:].rearrange("c (b n) -> c b n", b=B - 1),
                         x_v[:, 1:, :]).then_inc(s_xin[1], 16)
            sp.wait_ge(s_cstv, 2)
            sp.dma_start(slots.rearrange("(e p) w -> p e w", e=E)[0:TS, :, :],
                         pad_rows[:, :].unsqueeze(1).broadcast_to([P, E, RW])).then_inc(s_pre, 16)
            sp.sem_inc(s_free, TPI)
            with sp.Fori(0, NCH // TPI) as i:
                for c in range(TPI):
                    sp.wait_ge(s_scat[c], i * (16 * TOPK * NG) + 16 * TOPK * NG)
                    sp.sem_inc(s_free, 1)
            sp.wait_ge(s_tab, 1)
            sp.wait_ge(s_pre, 16)
            sp.wait_ge(s_scat[0], 16 * TOPK * NG * NCH // 2)
            sp.wait_ge(s_scat[1], 16 * TOPK * NG * NCH // 2)
            def load(off, i, j):
                sp.dma_start(xs[j % XB][:, :], slots[bass.DynSlice(off, TS), :]).then_inc(s_ld[j % XB], 16)

            def offsets(t, n):
                return nc.values_load_multi_w_load_instructions(
                    rowoff[0:1, bass.ds(t, n)], engines=(sp.engine,), min_val=0, max_val=E * CAP - TS,
                    skip_runtime_bounds_check_because=IN_RANGE)[1]

            for j0 in range(0, XB, 4):
                for j, off in enumerate(offsets(j0, 4)):
                    load(off, 0, j0 + j)

            def reload(i, j, off):
                t = i * XB + j
                sp.wait_ge(s_trx, t + 1)
                sp.wait_ge(s_ret, t + 1)
                load(off, i, j)

            for j, off in enumerate(offsets(XB, HEAD)):
                reload(0, j, off)
            with sp.Fori(0, LOOPS) as i:
                for j0 in range(HEAD, HEAD + XB, 4):
                    for j, off in enumerate(offsets(i * XB + j0 + XB, 4)):
                        reload(i, j0 + j, off)
            for b in range(XB):
                sp.wait_ge(s_ysc[b], 16 * len(range(b, NT, XB)))
            y_v = y_rows.rearrange("(k n p) d -> p k n d", k=TOPK, p=P)
            for b, (n0, n1) in enumerate(YB):
                for k in range(TOPK):
                    sp.dma_start(yk[:, k, n0 * C:n1 * C].rearrange("p (n d) -> p n d", d=C),
                                 y_v[:, k, n0:n1, :]).then_inc(s_yk[b], 16)
            for b in range(B):
                sp.wait_ge(s_fin, -(-(b + 1) * (TOK // B) // (FB * P)))
                sp.dma_start(out_v[:, b, :], fin[:, b * (TOK // B):(b + 1) * (TOK // B)]).then_inc(s_out, 16)
            sp.wait_ge(s_out, 16 * B)

        @block.gpsimd
        def _(pool):
            g = nc.gpsimd
            for free in (s_ids,):
                pool.sem_inc(free, CREDIT)
            g.memset(chunk_step[:, :, :], float(CT))
            g.memset(ident[:, :], 0.0).then_inc(s_cst, 1)
            g.memset(tri[:, :], 0.0).then_inc(s_cst, 1)
            g.memset(hmask[:, :], 1.0).then_inc(s_cst, 1)
            pool.wait_ge(s_cst, 3)
            g.affine_select(out=ident[:, :], in_=ident[:, :], compare_op=ALU.not_equal, fill=1.0,
                            base=0, pattern=[[-1, P]], channel_multiplier=1).then_inc(s_cst, 1)
            g.affine_select(out=tri[:, :], in_=tri[:, :], compare_op=ALU.is_ge, fill=1.0,
                            base=0, pattern=[[-1, GT]], channel_multiplier=1).then_inc(s_cst, 1)
            g.affine_select(out=hmask[:, :], in_=hmask[:, :], compare_op=ALU.is_ge, fill=0.0,
                            base=0, pattern=[[-HD, HEADS]], channel_multiplier=1).then_inc(s_cst, 1)
            pool.wait_ge(s_cst, 6)
            g.affine_select(out=hmask[:, :], in_=hmask[:, :], compare_op=ALU.is_ge, fill=0.0,
                            base=HD - 1, pattern=[[HD, HEADS]], channel_multiplier=-1).then_inc(s_cst, 1)
            exact = dict(allow_small_or_imprecise_dtypes=True)
            g.iota(iota_e[:, :], pattern=[[1, E]], base=0, channel_multiplier=0, **exact).then_inc(s_cst, 1)
            g.iota(ebase[:, :], pattern=[[CAP, E]], base=0, channel_multiplier=0, **exact).then_inc(s_cst, 1)
            g.iota(ids[:, :, :], pattern=[[TOK, TOPK], [GT, NG]], base=0, channel_multiplier=1,
                   **exact).then_inc(s_cst, 1)
            g.iota(iota_t[:, :], pattern=[[1, NT]], base=0, channel_multiplier=0, **exact).then_inc(s_cst, 1)
            g.iota(iota_p[:, :], pattern=[[0, 1]], base=0, channel_multiplier=1, **exact).then_inc(s_cst, 1)
            pool.wait_ge(s_pre, 16)
            with pool.Fori(0, NCH // TPI) as i:
                for c in range(TPI):
                    n = i * TPI + c
                    pool.wait_ge(s_rows, n + 1 + CREDIT)
                    pool.wait_ge(s_meta, n + 1)
                    g.tensor_tensor(ids[:, :, :], ids[:, :, :], chunk_step[:, :, :], ALU.add).then_inc(s_ids, 1)
                    for k in range(TOPK):
                        for gr in range(NG):
                            g.indirect_dma_start(
                                out=slots[:, :],
                                out_offset=bass.IndirectOffsetOnAxis(
                                    ap=dest[c][:, k * NG + gr:k * NG + gr + 1], axis=0),
                                in_=rows[c][:, k, gr, :], in_offset=None).then_inc(s_scat[c], 16)
            def scatter_outputs(i, j):
                b = j % XB
                pool.wait_ge(s_y, i * XB + j + 1)
                pool.sem_inc(s_carrier, 1)
                g.indirect_dma_start(
                    out=y_rows[:, :], out_offset=bass.IndirectOffsetOnAxis(ap=ret[b][:, 0:1], axis=0),
                    in_=y_sb[b][:, :], in_offset=None,
                    bounds_check=YROWS - 1, oob_is_err=False).then_inc(s_ysc[b], 16)

            tiles(pool, scatter_outputs)

        @block.scalar
        def _(act):
            a = nc.scalar
            for free in (s_km, s_rows, s_gx):
                act.sem_inc(free, CREDIT)
            act.dma_start(w_sb[:, :, 0:HID], w1.rearrange("e d h -> d e h")).then_inc(s_wl, 16)
            for f in range(NHALF):
                act.dma_start(w_sb[:, :, HID + f * C:HID + (f + 1) * C],
                              w2[:, f * P:(f + 1) * P, :].rearrange("e p d -> p e d")).then_inc(s_wl, 16)
            act.preload_act_table_set("natural_log_exp_and_others")
            act.wait_ge(s_cst, NCST)
            act.wait_ge(s_wtp, 1)
            a.activation(wT[:, :, :], bank(1).rearrange("p (a c) -> p a c", a=4), ACT.Copy).then_inc(s_wt, 1)
            act.wait_ge(s_wtp, 2)
            a.activation(wgc[:, :], bank(0, E), ACT.Copy).then_inc(s_wt, 1)

            def norm_q_k_v(n, c):
                act.wait_ge(s_km, n + CREDIT)
                act.wait_ge(s_xc, n + 1)
                a.activation(sq[c][:, :], bank(XC_K, CT), ACT.Square).then_inc(s_sq, 1)

            def channel_rstd(n):
                act.wait_ge(s_var, n + 1)
                act.wait_ge(s_xn, n + CREDIT)
                a.activation(lnv[:, :], bank(VAR_Q, CT), ACT.Ln, bias=eps_c[:, 0:1]).then_inc(s_lnv, 1)
                act.wait_ge(s_lnv, n + 1)
                a.activation(rstd[:, :], lnv[:, :], ACT.Exp, scale=-0.5).then_inc(s_rs, 1)

            def token_rstd(n):
                act.wait_ge(s_bmv, n + 1)
                a.activation(lnv2[:, :], bmv[:, :, 1], ACT.Ln, bias=eps_t[0:GT, 0:1]).then_inc(s_lnv2, 1)
                act.wait_ge(s_lnv2, n + 1)
                a.activation(rstd2[:, :], lnv2[:, :], ACT.Exp, scale=-0.5).then_inc(s_rs2, 1)

            def masked_keys(n, c):
                act.wait_ge(s_kp, n + 1)
                for hq in range(HQ):
                    last = a.activation(km[c][:, hq, :], bank(XC_K, CT), ACT.Identity,
                                        bias=zero_c[:, 0:1], scale=kmask[:, hq:hq + 1])
                last.then_inc(s_km, 1)

            def values(n, c):
                act.wait_ge(s_vp, n + 1)
                a.activation(vs[c][:, :], bank(V_B, NG * C), ACT.Copy).then_inc(s_vs, 1)

            def exps(n, c):
                act.wait_ge(s_sub, n + 1 + CREDIT)
                a.activation(ex[c][:, :, 0:W], es[c][:, :, :], ACT.Exp).then_inc(s_e, 1)

            def first_heads(n, c):
                act.wait_ge(s_av, n + 1)
                a.activation(av0[:, :].rearrange("p (r n) -> p r n", r=RG), av_view[:, :, 0, :], ACT.Identity,
                             bias=zero_c[:, 0:1], scale=pmask[:, 0:1]).then_inc(s_av0, 1)

            def keep_t(n, c):
                act.wait_ge(s_t, n + 1 + CREDIT)
                a.activation(t_sb[:, bass.ds(n * CT, CT)], tc[c][:, :], ACT.Copy).then_inc(s_tcp, 1)

            def normed_rows(n, c):
                act.wait_ge(s_st, n + 1)
                act.wait_ge(s_free, n + 1)
                for k in range(TOPK):
                    for gr in range(NG):
                        last = a.activation(rows[c][:, k, gr, 0:C],
                                            ps[0:GT, TR_B * 512 + gr * P:TR_B * 512 + gr * P + C], ACT.Identity,
                                            bias=nmr[:, gr:gr + 1], scale=rstd2[:, gr:gr + 1])
                last.then_inc(s_rows, 1)

            def gate_exps(n, c):
                act.wait_ge(s_m0, n + 1)
                for gr in range(NG):
                    a.activation(junk[:, gr, :], lg[:, gr, :], ACT.Exp, bias=nm0[:, gr:gr + 1],
                                 accum_out=esum[:, gr:gr + 1])
                a.activation(e2[:, :], dm[:, :], ACT.Exp).then_inc(s_gx, 1)

            def chunk(n, c, more):
                o = 1 - c
                if more:
                    norm_q_k_v(n + 1, o)
                    channel_rstd(n + 1)
                first_heads(n, c)
                if more:
                    masked_keys(n + 1, o)
                keep_t(n, c)
                token_rstd(n)
                if more:
                    values(n + 1, o)
                normed_rows(n, c)
                if more:
                    exps(n + 1, o)
                gate_exps(n, c)

            act.wait_ge(s_cstv, 2)
            norm_q_k_v(0, 0)
            channel_rstd(0)
            masked_keys(0, 0)
            values(0, 0)
            exps(0, 0)
            with act.Fori(0, NCH // TPI - 1) as i:
                for c in range(TPI):
                    chunk(i * TPI + c, c, True)
            for c in range(TPI):
                chunk(NCH - TPI + c, c, c + 1 < TPI)

            def take_xT(i, j):
                act.wait_ge(s_trx, i * XB + j + 1)
                a.activation(xT[j % 2][:, :], bank(j % 2, TS), ACT.Copy).then_inc(s_xT, 1)

            def gelu(i, j):
                act.wait_ge(s_h, i * XB + j + 1)
                a.activation(hT[j % 2][:, :, :].rearrange("p f s -> p (f s)"), bank(2 + j % 2, HID),
                             ACT.Gelu).then_inc(s_g, 1)

            def tile(i, j):
                last = isinstance(i, int)
                if not last or j + 2 < NT:
                    take_xT(i, j + 2)
                if not last or j + 1 < NT:
                    gelu(i, j + 1)

            take_xT(0, 0)
            take_xT(0, 1)
            gelu(0, 0)
            tiles(act, tile)

        @block.vector
        def _(dve):
            v = nc.vector
            for free in (s_xn, s_q, s_o, s_sub, s_t, s_pb, s_macc):
                dve.sem_inc(free, CREDIT)
            v.memset(zero_c[:, :], 0.0)
            v.memset(eps_c[:, :], EPS_C)
            v.memset(eps_t[:, :], EPS_T)
            v.memset(pad_rows[:, :], 0.0).then_inc(s_cstv, 1)
            dve.wait_ge(s_cstv, 1)
            v.memset(pad_rows[:, ID:ID + 1].bitcast(I32), SKIP)
            v.memset(avg[:, :], 1.0 / C)
            v.memset(ones[:, :], 1.0)
            v.memset(one_e[:, :], 1.0)
            v.memset(macc[:, :], 0.0)
            v.memset(maccb[:, :], 0.0)
            v.memset(past[:, :, 0:1], 1.0)
            for c in range(2):
                v.memset(xn[c][:, :], 0.0)
                v.memset(qs[c][:, :], 0.0)
                v.memset(ex[c][:, :, :], 0.0)
                v.memset(rows[c][:, :, :, C:], 0.0)
            dve.wait_ge(s_cst, NCST)
            for f in range(HF):
                v.tensor_scalar(hscale[:, f, :], hmask[:, f * HQ:(f + 1) * HQ], SCALE, None,
                                ALU.mult).then_inc(s_masks, 1)
            v.tensor_reduce(pmask[:, :], hmask[:, :].rearrange("c (p a) -> c a p", a=2), AX.X,
                            ALU.add).then_inc(s_masks, 1)
            dve.wait_ge(s_masks, 3)
            v.tensor_tensor(kmask[:, :], hscale[:, 0, :], hscale[:, 1, :], ALU.add)
            v.tensor_scalar(cmat[:, :], ident[:, :], -1.0 / C, None, ALU.add).then_inc(s_cstv, 1)
            def layer_norm(n, c):
                dve.wait_ge(s_rs, n + 1)
                v.tensor_tensor(xn[c][:, :].rearrange("p (a w) -> p a w", w=WP)[:, :, 0:W],
                                bank(XC_K, CT).rearrange("p (a w) -> p a w", w=W),
                                rstd[:, :].rearrange("p (a w) -> p a w", w=W), ALU.mult).then_inc(s_xn, 1)

            def queries(n, c):
                dve.wait_ge(s_qp, n + 1)
                v.tensor_copy(qs[c][:, :].rearrange("p (a w) -> p a w", w=WP)[:, :, 0:W],
                              bank(VAR_Q, CT).rearrange("p (a w) -> p a w", w=W)).then_inc(s_q, 1)

            NS = HF * NG * HQ

            def row_max(n, c):
                dve.wait_ge(s_s, n + 1)
                v.tensor_reduce(mx[:, :].rearrange("p (f a) -> p f a", f=HF), s_view, AX.X,
                                ALU.max).then_inc(s_mx, 1)
                dve.wait_ge(s_mx, n + 1)
                v.tensor_tensor(es[c][:, :, :].rearrange("p (f a) j -> p f a j", f=HF), s_view,
                                mx[:, :].rearrange("p (f a) -> p f a", f=HF).unsqueeze(3)
                                .broadcast_to([P, HF, NG * HQ, W]), ALU.subtract).then_inc(s_sub, 1)

            def row_sum(n, c):
                dve.wait_ge(s_e, n + 1)
                v.tensor_reduce(den[:, :], ex[c][:, :, 0:W], AX.X, ALU.add).then_inc(s_den, 1)

            def normalise(n, c):
                dve.wait_ge(s_den, n + 1)
                v.reciprocal(rden[:, :], den[:, :]).then_inc(s_rden, 1)

            def spread(n, c):
                dve.wait_ge(s_rden, n + 1)
                v.tensor_tensor(ex[c][:, :, 0:W], ex[c][:, :, 0:W],
                                rden[:, :].unsqueeze(2).broadcast_to([P, NS, W]), ALU.mult).then_inc(s_nrm, 1)
                dve.wait_ge(s_nrm, n + 1)
                v.transpose(exT[c][:, :, :].rearrange("p a w -> p (a w)"),
                            ex[c][:, :, :].rearrange("p a w -> p (a w)")).then_inc(s_et, 1)

            def attn_out(n, c):
                dve.wait_ge(s_av0, n + 1)
                v.scalar_tensor_tensor(o_sb[c][:, :].rearrange("p (r n) -> p r n", r=RG), av_view[:, :, 1, :],
                                       pmask[:, 1:2], av0[:, :].rearrange("p (r n) -> p r n", r=RG),
                                       ALU.mult, ALU.add).then_inc(s_o, 1)

            def residual(n, c):
                dve.wait_ge(s_pj, n + 1)
                v.scalar_tensor_tensor(tc[c][:, :], bank(PJ_B, CT), bo[:, 0:1], x_sb[:, bass.ds(n * CT, CT)],
                                       ALU.add, ALU.add).then_inc(s_t, 1)

            def token_stats(n, c):
                dve.wait_ge(s_tr, n + 1)
                for gr in range(NG):
                    last = v.bn_stats(bst[:, gr, :], ps[0:GT, TR_B * 512 + gr * P:TR_B * 512 + gr * P + C])
                last.then_inc(s_bst, 1)
                dve.wait_ge(s_win, 64)
                dve.wait_ge(s_bst, n + 1)
                dve.wait_ge(s_rows, n + CREDIT)
                for gr in range(NG):
                    last = v.bn_aggr(bmv[:, gr, :], bst[:, gr, :])
                last.then_inc(s_bmv, 1)
                dve.wait_ge(s_bmv, n + 1)
                dve.wait_ge(s_rs2, n + 1)
                v.scalar_tensor_tensor(nmr[:, :], bmv[:, :, 0], -1.0, rstd2[:, :], ALU.mult,
                                       ALU.mult).then_inc(s_st, 1)

            def top2(n, c):
                dve.wait_ge(s_lg, n + 1)
                dve.wait_ge(s_gx, n + CREDIT)
                v.tensor_tensor(lg[:, :, :], LG.rearrange("p (g e) -> p g e", g=NG),
                                rstd2[:, :].unsqueeze(2).broadcast_to([GT, NG, E]), ALU.mult).then_inc(s_lgs, 1)
                dve.wait_ge(s_win, 64)
                dve.wait_ge(s_lgs, n + 1)
                for gr in range(NG):
                    last = v.max(m8[:, gr, :], lg[:, gr, :])
                last.then_inc(s_m8, 1)
                dve.wait_ge(s_win, 64)
                dve.wait_ge(s_m8, n + 1)
                for gr in range(NG):
                    last = v.max_index(i8[:, gr, :], m8[:, gr, :], lg[:, gr, :])
                last.then_inc(s_i8, 1)
                v.tensor_tensor(dm[:, :], m8[:, :, 1], m8[:, :, 0], ALU.subtract)
                v.tensor_scalar(nm0[:, :], m8[:, :, 0], -1.0, None, ALU.mult).then_inc(s_m0, 1)
                dve.wait_ge(s_i8, n + 1)
                v.tensor_copy(idx[:, :, :], i8[:, :, 0:TOPK].rearrange("p g k -> p k g")).then_inc(s_idx, 1)
                dve.wait_ge(s_idx, n + 1)
                v.tensor_tensor(oh[:, :, :].rearrange("p k (g e) -> p (k g) e", e=E),
                                iota_e[0:GT, :].unsqueeze(1).broadcast_to([GT, TOPK * NG, E]),
                                idx[:, :, :].rearrange("p k g -> p (k g)").unsqueeze(2)
                                .broadcast_to([GT, TOPK * NG, E]), ALU.is_equal).then_inc(s_oh, 1)
                dve.wait_ge(s_oh, n + 1)
                v.tensor_tensor(mt[:, :, :].rearrange("p g e -> p (g e)"), oh[:, 0, :], oh[:, 1, :],
                                ALU.add).then_inc(s_mt, 1)

            def slot_rows(n, c):
                dve.wait_ge(s_mt, n + 1)
                v.tensor_reduce(msum[:, :], mt[:, :, :].rearrange("p g e -> p e g"), AX.X,
                                ALU.add).then_inc(s_ms, 1)
                dve.wait_ge(s_pos, n + 1)
                v.tensor_tensor(posb[:, :].rearrange("p (g e) -> p g e", g=NG),
                                POS.rearrange("p (g e) -> p g e", g=NG),
                                ebase[0:GT, :].unsqueeze(1).broadcast_to([GT, NG, E]), ALU.add).then_inc(s_pb, 1)
                dve.wait_ge(s_ms, n + 1)
                v.tensor_tensor(macc[:, :], macc[:, :], msum[:, :], ALU.add).then_inc(s_ma, 1)
                dve.wait_ge(s_pb, n + 1 + CREDIT)
                v.tensor_tensor(prod[:, :, :], oh[:, :, :], posb[:, :].unsqueeze(1)
                                .broadcast_to([GT, TOPK, NG * E]), ALU.mult).then_inc(s_pr, 1)
                dve.wait_ge(s_ma, n + 1)
                v.tensor_copy(maccb[:, :], macc[:, :]).then_inc(s_macc, 1)
                dve.wait_ge(s_pr, n + 1)
                v.tensor_reduce(destf[:, :], prod[:, :, :].rearrange("p k (g e) -> p (k g) e", e=E), AX.X,
                                ALU.add).then_inc(s_df, 1)
                dve.wait_ge(s_gx, n + 1 + CREDIT)
                v.reciprocal(rg[:, :], esum[:, :]).then_inc(s_rg, 1)
                dve.wait_ge(s_free, n + 1)
                dve.wait_ge(s_df, n + 1)
                v.tensor_copy(dest[c][:, :], destf[:, :])
                dve.wait_ge(s_ids, n + CREDIT)
                v.tensor_copy(rows[c][:, :, :, ID].bitcast(U32), ids[:, :, :])
                dve.wait_ge(s_rg, n + 1)
                v.tensor_copy(rows[c][:, 0, :, GATE], rg[:, :])
                v.tensor_tensor(rows[c][:, 1, :, GATE], rg[:, :], e2[:, :], ALU.mult).then_inc(s_meta, 1)

            def chunk(n, c, more):
                o = 1 - c
                if more:
                    layer_norm(n + 1, o)
                attn_out(n, c)
                if more:
                    queries(n + 1, o)
                residual(n, c)
                token_stats(n, c)
                if more:
                    row_max(n + 1, o)
                top2(n, c)
                if more:
                    row_sum(n + 1, o)
                    normalise(n + 1, o)
                    spread(n + 1, o)
                slot_rows(n, c)

            dve.wait_ge(s_win, 64)
            layer_norm(0, 0)
            queries(0, 0)
            row_max(0, 0)
            row_sum(0, 0)
            normalise(0, 0)
            spread(0, 0)
            with dve.Fori(0, NCH // TPI - 1) as i:
                for c in range(TPI):
                    chunk(i * TPI + c, c, True)
            for c in range(TPI):
                chunk(NCH - TPI + c, c, c + 1 < TPI)

            step = [0]

            def then(ins):
                step[0] += 1
                ins.then_inc(s_v, 1)
                dve.wait_ge(s_v, step[0])

            dve.wait_ge(s_cnt, 1)
            then(v.tensor_copy(cnt[:, :], CNT))
            then(v.tensor_scalar(nt_i[:, :], cnt[:, :], float(TS - 1), None, ALU.add))
            then(v.tensor_scalar(nt_i[:, :], nt_i[:, :], TS.bit_length() - 1, None, ALU.logical_shift_right))
            then(v.tensor_copy(nt_f[:, :], nt_i[:, :]))
            then(v.tensor_tensor_scan(ct_f[:, :], one_e[:, :], nt_f[:, :], 0.0, ALU.mult, ALU.add))
            shape = [P, NT, E]
            then(v.tensor_tensor(past[:, :, 1:E + 1], iota_t[:, :].unsqueeze(2).broadcast_to(shape),
                                 ct_f[:, :].unsqueeze(1).broadcast_to(shape), ALU.is_ge))
            then(v.tensor_reduce(e_t[:, :], past[:, :, 1:E + 1], AX.X, ALU.add))
            then(v.tensor_tensor(tw[:, :, :], past[:, :, 1:E + 1], nt_f[:, :].unsqueeze(1).broadcast_to(shape),
                                 ALU.mult))
            then(v.tensor_reduce(first[:, :], tw[:, :, :], AX.X, ALU.add))
            then(v.tensor_tensor(tw[:, :, :], past[:, :, 0:E], past[:, :, 1:E + 1], ALU.subtract))
            then(v.tensor_tensor(tw[:, :, :], tw[:, :, :], cnt[:, :].unsqueeze(1).broadcast_to(shape), ALU.mult))
            then(v.tensor_reduce(c_t[:, :], tw[:, :, :], AX.X, ALU.add))
            then(v.tensor_tensor(j128[:, :], iota_t[:, :], first[:, :], ALU.subtract))
            then(v.tensor_scalar(j128[:, :], j128[:, :], float(TS), None, ALU.mult))
            then(v.scalar_tensor_tensor(start[:, :], c_t[:, :], -float(TS), j128[:, :], ALU.add, ALU.min))
            then(v.tensor_scalar(start[:, :], start[:, :], 0.0, None, ALU.max))
            then(v.tensor_scalar(skip[:, :], e_t[:, :], float(E), float(TS), ALU.is_equal, ALU.mult))
            then(v.tensor_tensor(skip[:, :], skip[:, :], j128[:, :], ALU.add))
            then(v.tensor_tensor(skip[:, :], skip[:, :], start[:, :], ALU.subtract))
            then(v.tensor_scalar(skip[:, :], skip[:, :], iota_p[:, 0:1], float(SKIP), ALU.is_gt, ALU.mult))
            then(v.tensor_scalar(e_c[:, :], e_t[:, :], float(E - 1), None, ALU.min))
            v.tensor_scalar(woff[:, :], e_c[:, :], float(HID + NHALF * C), None, ALU.mult)
            v.scalar_tensor_tensor(rowoff[:, :], e_c[:, :], float(CAP), start[:, :], ALU.mult,
                                   ALU.add).then_inc(s_tab, 1)
            dve.wait_ge(s_tab, 1)

            def ahead(off, i, j):
                b = j % XB
                dve.wait_ge(s_ld[b], used(i, j))
                if j >= XB:
                    dve.wait_ge(s_ysc[b], used(i, j - XB))
                elif not isinstance(i, int):
                    dve.wait_ge(s_ysc[b], i * 16)
                v.tensor_copy(gate[b][:, :], xs[b][:, GATE:GATE + 1])
                v.tensor_tensor(ret[b][:, :], xs[b][:, ID:ID + 1].bitcast(U32), skip[:, bass.ds(i * XB + j, 1)],
                                ALU.add).then_inc(s_ret, 1)
                v.tensor_copy(we[j % WB][:, :], w_flat[:, bass.ds(off, HID + NHALF * C)]).then_inc(s_we, 1)

            def expert_offsets(t, n):
                return nc.values_load_multi_w_load_instructions(
                    woff[0:1, bass.ds(t, n)], engines=(dve.engine,), min_val=0,
                    max_val=(E - 1) * (HID + NHALF * C), skip_runtime_bounds_check_because=IN_RANGE)[1]

            def tile(i, j, off):
                b = j % XB
                if off is not None:
                    ahead(off, i, j + 2)
                dve.wait_ge(s_yp, i * XB + j + 1)
                v.tensor_scalar(y_sb[b][:, :], bank(6 + j % 2, C), gate[b][:, :], None,
                                ALU.mult).then_inc(s_y, 1)

            dve.wait_ge(s_wl, 16 * (1 + NHALF))
            w_flat = w_sb[:, :, :].rearrange("p e n -> p (e n)")
            offs = expert_offsets(0, HEAD + 2)
            ahead(offs[0], 0, 0)
            ahead(offs[1], 0, 1)
            for j in range(HEAD):
                tile(0, j, offs[j + 2])
            with dve.Fori(0, LOOPS) as i:
                for j0 in range(HEAD, HEAD + XB, 4):
                    for j, off in enumerate(expert_offsets(i * XB + j0 + 2, 4)):
                        tile(i, j0 + j, off)
            t0 = HEAD + LOOPS * XB
            for j0 in range(t0, NT, 4):
                offs = expert_offsets(j0 + 2, min(4, NT - j0 - 2))
                for j in range(4):
                    tile(0, j0 + j, offs[j] if j < len(offs) else None)

            for b, (n0, n1) in enumerate(YB):
                dve.wait_ge(s_yk[b], 16 * TOPK)
                v.tensor_tensor(ysum[:, n0 * C:n1 * C], yk[:, 0, n0 * C:n1 * C], yk[:, 1, n0 * C:n1 * C],
                                ALU.add).then_inc(s_ys, 1)
            for b, (n0, n1) in enumerate(YB):
                dve.wait_ge(s_yt, b + 1)
                v.tensor_tensor(fin[:, n0 * P:n1 * P], ps[:, n0 * P:n1 * P], t_sb[:, n0 * P:n1 * P],
                                ALU.add).then_inc(s_fin, 1)

        @block.tensor
        def _(pe):
            mm = nc.tensor.matmul
            pe.wait_ge(s_cst, NCST)
            pe.wait_ge(s_win, 64)
            for k in range(3):
                nc.tensor.transpose(ps[:, 512 + k * C:512 + (k + 1) * C], wqkv_sb[:, k, :], ident[:, :])
            nc.tensor.transpose(ps[:, 512 + 3 * C:512 + 4 * C], wout_sb[:, :], ident[:, :]).then_inc(s_wtp, 1)
            pe.wait_ge(s_cstv, 2)
            mm(bank(0, E), cmat[:, :], wg[:, :], start=True, stop=True).then_inc(s_wtp, 1)
            pe.wait_ge(s_wt, 2)
            pe.wait_ge(s_xin[0], 16)

            def centre(n):
                pe.wait_ge(s_km, n + CREDIT)
                mm(bank(XC_K, CT), cmat[:, :], x_sb[:, bass.ds(n * CT, CT)], start=True,
                   stop=True).then_inc(s_xc, 1)

            def variance(n, c):
                pe.wait_ge(s_sq, n + 1)
                pe.wait_ge(s_q, n + CREDIT)
                mm(bank(VAR_Q, CT), avg[:, :], sq[c][:, :], start=True, stop=True).then_inc(s_var, 1)

            def project(n, c):
                pe.wait_ge(s_xn, n + 1 + CREDIT)
                xr = xn[c][:, :].rearrange("p (a w) -> p a w", w=WP)[:, :, 0:W]
                mm(bank(VAR_Q, CT), wT[:, 0, :], xr, start=True, stop=True).then_inc(s_qp, 1)
                mm(bank(XC_K, CT), wT[:, 1, :], xr, start=True, stop=True).then_inc(s_kp, 1)

            def value_rows(n, c):
                pe.wait_ge(s_o, n + CREDIT)
                for gr in range(NG):
                    last = mm(ps[:, V_B * 512 + gr * C:V_B * 512 + (gr + 1) * C], xn[c][:, gr * P:(gr + 1) * P],
                              wT[:, 2, :], start=True, stop=True)
                last.then_inc(s_vp, 1)

            def scores(n, c):
                pe.wait_ge(s_wt, 2)
                pe.wait_ge(s_q, n + 1 + CREDIT)
                pe.wait_ge(s_km, n + 1 + CREDIT)
                pe.wait_ge(s_sub, n + CREDIT)
                for gr in range(NG):
                    for r in range(RG):
                        row = gr * RG + r
                        for f in range(HF):
                            col = (S0 + f) * 512 + gr * HQ * W
                            last = mm(ps[r * 32:(r + 1) * 32, col:col + HQ * W],
                                      qs[c][f * 64:(f + 1) * 64, row * WP:(row + 1) * WP],
                                      km[c][f * 64:(f + 1) * 64, :, row * W:(row + 1) * W],
                                      start=True, stop=True)
                last.then_inc(s_s, 1)

            def attend(n, c):
                pe.wait_ge(s_wt, 2)
                pe.wait_ge(s_et, n + 1)
                pe.wait_ge(s_vs, n + 1)
                pe.wait_ge(s_t, n + CREDIT)
                pe.wait_ge(s_rows, n + CREDIT)
                pe.wait_ge(s_pb, n + CREDIT)
                for gr in range(NG):
                    for p in range(NP):
                        for r in range(RG):
                            a0 = (2 * p // HQ) * NG * HQ + gr * HQ + 2 * p % HQ
                            out_ap = av_view[p * 32:(p + 1) * 32, r, :, gr * W:(gr + 1) * W]
                            last = mm(out_ap,
                                      vs[c][r * 32:(r + 1) * 32, gr * C + p * 32:gr * C + (p + 1) * 32],
                                      exT[c][r * 32:(r + 1) * 32, a0:a0 + 2, 0:W], start=True, stop=True)
                last.then_inc(s_av, 1)

            def out_proj(n, c):
                pe.wait_ge(s_o, n + 1 + CREDIT)
                mm(bank(PJ_B, CT), wT[:, 3, :],
                   o_sb[c][:, :].rearrange("p (r g i) -> p g r i", r=RG, g=NG), start=True, stop=True).then_inc(s_pj, 1)

            def token_major(n, c):
                pe.wait_ge(s_t, n + 1 + CREDIT)
                for gr in range(NG):
                    last = nc.tensor.transpose(ps[0:GT, TR_B * 512 + gr * P:TR_B * 512 + gr * P + C],
                                               tc[c][:, gr * GT:(gr + 1) * GT], ident[:, :])
                last.then_inc(s_tr, 1)
                for gr in range(NG):
                    last = mm(LG[:, gr * E:(gr + 1) * E], tc[c][:, gr * GT:(gr + 1) * GT], wgc[:, :],
                              start=True, stop=True)
                last.then_inc(s_lg, 1)

            def places(n):
                pe.wait_ge(s_macc, n + CREDIT)
                pe.wait_ge(s_mt, n + 1)
                for gr in range(NG):
                    col = POS[:, gr * E:(gr + 1) * E]
                    mm(col, ones[:, 0:GT], maccb[:, :], start=True, stop=False)
                    for before in range(gr):
                        mm(col, ones[:, 0:GT], mt[:, before, :], start=False, stop=False)
                    last = mm(col, tri[:, :], mt[:, gr, :], start=False, stop=True)
                last.then_inc(s_pos, 1)

            def chunk(n, c, more):
                o = 1 - c
                if more:
                    centre(n + 1)
                attend(n, c)
                if more:
                    variance(n + 1, o)
                    project(n + 1, o)
                out_proj(n, c)
                if more:
                    value_rows(n + 1, o)
                token_major(n, c)
                if more:
                    scores(n + 1, o)
                places(n)

            centre(0)
            variance(0, 0)
            project(0, 0)
            value_rows(0, 0)
            scores(0, 0)
            pe.wait_ge(s_xin[1], 16)
            with pe.Fori(0, NCH // TPI - 1) as i:
                for c in range(TPI):
                    chunk(i * TPI + c, c, True)
            for c in range(TPI):
                chunk(NCH - TPI + c, c, c + 1 < TPI)
            pe.wait_ge(s_macc, NCH + CREDIT)
            mm(CNT, ones[:, :], maccb[:, :], start=True, stop=True).then_inc(s_cnt, 1)

            def rows_T(i, j):
                pe.wait_ge(s_ld[j % XB], used(i, j))
                nc.tensor.transpose(bank(j % 2, TS), xs[j % XB][:, 0:C], ident[:, :]).then_inc(s_trx, 1)

            def hidden(i, j):
                pe.wait_ge(s_we, i * XB + j + 1)
                pe.wait_ge(s_xT, i * XB + j + 1)
                for f in range(NHALF):
                    last = mm(ps[:, (2 + j % 2) * 512 + f * TS:(2 + j % 2) * 512 + (f + 1) * TS],
                              we[j % WB][:, f * P:(f + 1) * P], xT[j % 2][:, :], start=True, stop=True)
                last.then_inc(s_h, 1)

            def outputs(i, j):
                if isinstance(i, int) and j == NT - 1:
                    pe.wait_ge(s_y, NT - 2)
                pe.wait_ge(s_g, i * XB + j + 1)
                for f in range(NHALF):
                    last = mm(bank(6 + j % 2, C), hT[j % 2][:, f, :],
                              we[j % WB][:, HID + f * C:HID + (f + 1) * C], start=(f == 0), stop=(f == NHALF - 1))
                last.then_inc(s_yp, 1)

            def tile(i, j):
                last = isinstance(i, int)
                if not last or j + 2 < NT:
                    rows_T(i, j + 2)
                if not last or j + 1 < NT:
                    hidden(i, j + 1)
                outputs(i, j)

            rows_T(0, 0)
            rows_T(0, 1)
            hidden(0, 0)
            tiles(pe, tile)

            pe.wait_ge(s_y, NT)
            for b, (n0, n1) in enumerate(YB):
                pe.wait_ge(s_ys, b + 1)
                for m in range(n0, n1):
                    last = nc.tensor.transpose(ps[:, m * P:(m + 1) * P], ysum[:, m * C:(m + 1) * C], ident[:, :])
                last.then_inc(s_yt, 1)


_INS = ["x", "L0_conv_w_qkv", "L0_conv_w_out", "L0_conv_b_out", "L0_ffn_W_gate", "L0_ffn_W1", "L0_ffn_W2"]


def kernel(**inputs):
    import concourse.bacc as bacc
    from concourse.bass_utils import run_bass_kernel_spmd

    nc = bacc.Bacc("TRN2", target_bir_lowering=False, num_devices=1)
    arrays, args = {}, []
    for name in _INS:
        a = np.ascontiguousarray(inputs[name])
        arrays[f"in_{name}"] = a
        args.append(nc.dram_tensor(f"in_{name}", a.shape, mybir.dt.from_np(a.dtype), kind="ExternalInput").ap())
    out = nc.dram_tensor("out_x", (B, C, H, W), F32, kind="ExternalOutput").ap()
    build(nc, *args, out)
    r = run_bass_kernel_spmd(nc, [arrays], core_ids=[0])
    return r.results[0]["out_x"]
```

```python
from contextlib import ExitStack

import numpy as np
import concourse.bass as bass
from concourse import mybir

F32 = mybir.dt.float32
BF16 = mybir.dt.bfloat16
I32 = mybir.dt.int32
U32 = mybir.dt.uint32
ALU = mybir.AluOpType
ACT = mybir.ActivationFunctionType
AX = mybir.AxisListType

P = 128
B, C, H, W = 4, 128, 24, 24
HEADS = 8
HD = C // HEADS
SCALE = HD ** -0.5
E = 16
HID = 256
NHALF = HID // P
EPS_C = 1e-6
EPS_T = 1e-5
TOK = B * H * W

RG = 4
WP = 32
GT = RG * W
NG = 3
CT = NG * GT
CR = NG * RG
NCH = TOK // CT
HF = 2
HQ = HEADS // HF
NP = HEADS // 2
TOPK = 2

TS = 128
CAP = TOK + TS
RW = C + 4
ID, GATE = C, C + 1
NT = (TOPK * TOK + E * (TS - 1)) // TS + 1
XB = 8
WB = 4
HEAD = NT % XB
LOOPS = NT // XB - 1
YROWS = TOPK * TOK
WARM = 10
IN_RANGE = "clamped where the tile table is worked out"
SKIP = 8192


def build(nc, x, w_qkv, w_out, b_out, w_gate, w1, w2, out):
    x_v = x.rearrange("b c h w -> c b (h w)")
    out_v = out.rearrange("b c h w -> c b (h w)")
    slots = nc.dram_tensor("slots", (E * CAP, RW), F32, kind="Internal").ap()
    y_rows = nc.dram_tensor("y_rows", (YROWS, C), F32, kind="Internal").ap()

    ctx = ExitStack()
    with ctx:
        def sb(name, shape, dt=F32):
            return ctx.enter_context(nc.sbuf_tensor(name, shape, dt))

        def sem(name):
            return ctx.enter_context(nc.semaphore(name))

        x_sb = sb("x_sb", [P, TOK])
        t_sb = sb("t_sb", [P, TOK])
        wqkv_sb = sb("wqkv_sb", [P, 3, C])
        wout_sb = sb("wout_sb", [P, C])
        wT = sb("wT", [P, 4, C])
        bo = sb("bo", [P, 1])
        wg = sb("wg", [P, E])
        w_sb = sb("w_sb", [P, E, HID + NHALF * C])
        id_wg = sb("id_wg", [P, P + E])
        ident, wgc = id_wg[:, 0:P], id_wg[:, P:]
        cmat = sb("cmat", [P, P])
        avg = sb("avg", [P, P])
        tri = sb("tri", [GT, GT], BF16)
        ones = sb("ones", [GT, P], BF16)
        hmask = sb("hmask", [P, HEADS])
        kmask = sb("kmask", [P, HQ])
        hscale = sb("hscale", [P, HF, HQ])
        pmask = sb("pmask", [P, 2])
        iota_e = sb("iota_e", [P, E])
        ebase = sb("ebase", [P, E])
        ids = sb("ids", [GT, TOPK, NG])
        chunk_step = sb("chunk_step", [GT, TOPK, NG])
        zero_c = sb("zero_c", [P, 1])
        eps_c = sb("eps_c", [P, 1])
        eps_t = sb("eps_t", [P, 1])
        lnv = sb("lnv", [P, CT])
        lnv2 = sb("lnv2", [GT, NG])
        zeros = sb("zeros", [P, 512], BF16)
        pad_rows = sb("pad_rows", [P, RW])
        padid = sb("padid", [P, 1])

        sq = [sb(f"sq{i}", [P, CT]) for i in range(2)]
        rstd = sb("rstd", [P, CT])
        xn = [sb(f"xn{i}", [P, CR * WP]) for i in range(2)]
        qs = [sb(f"qs{i}", [P, CR * WP]) for i in range(2)]
        km = [sb(f"km{i}", [P, HQ, CT]) for i in range(2)]
        vs = [sb(f"vs{i}", [P, NG * C]) for i in range(2)]
        mx = sb("mx", [P, HF * NG * HQ])
        den = sb("den", [P, HF * NG * HQ])
        rden = sb("rden", [P, HF * NG * HQ])
        es = [sb(f"es{i}", [P, HF * NG * HQ, W]) for i in range(2)]
        ex = [sb(f"ex{i}", [P, HF * NG * HQ, WP]) for i in range(2)]
        exT = [sb(f"exT{i}", [P, HF * NG * HQ, WP]) for i in range(2)]
        av0 = sb("av0", [P, CT])
        o_sb = [sb(f"o_sb{i}", [P, CT]) for i in range(2)]
        tc = [sb(f"tc{i}", [P, CT]) for i in range(2)]
        bst = sb("bst", [GT, NG, 6])
        bmv = sb("bmv", [GT, NG, 2])
        nmr = sb("nmr", [GT, NG])
        rstd2 = sb("rstd2", [GT, NG])
        rows = [sb(f"rows{i}", [GT, TOPK, NG, RW]) for i in range(2)]
        lg = sb("lg", [GT, NG, E])
        m8 = sb("m8", [GT, NG, 8])
        i8 = sb("i8", [GT, NG, 8], U32)
        idx = sb("idx", [GT, TOPK, NG])
        nm0 = sb("nm0", [GT, NG])
        dm = sb("dm", [GT, NG])
        junk = sb("junk", [GT, NG, E])
        tl_sb = sb("tl_sb", [GT, NG * (C + E)])
        esum = sb("esum", [GT, NG])
        e2 = sb("e2", [GT, NG])
        oh = sb("oh", [GT, TOPK, NG * E])
        mt = sb("mt", [GT, NG, E], BF16)
        msum = sb("msum", [GT, E])
        macc = sb("macc", [GT, E])
        maccb = sb("maccb", [GT, E], BF16)
        posb = sb("posb", [GT, NG * E])
        prod = sb("prod", [GT, TOPK, NG * E])
        destf = sb("destf", [GT, TOPK * NG])
        dest = [sb(f"dest{i}", [GT, TOPK * NG], U32) for i in range(2)]
        rg = sb("rg", [GT, NG])

        iota_p = sb("iota_p", [P, 1])
        iota_s = sb("iota_s", [P, 1])
        cnt = sb("cnt", [P, E])
        nt_i = sb("nt_i", [P, E], I32)
        nt_f = sb("nt_f", [P, E])
        ct_f = sb("ct_f", [P, E])
        one_e = sb("one_e", [P, E])
        facts = sb("facts", [P, 3, E + 1])
        mine = sb("mine", [P, E])
        sums3 = sb("sums3", [P, 3])
        list_row = sb("list_row", [P, 1])
        start = sb("start", [P, 1])
        e_c = sb("e_c", [P, 1])
        none = sb("none", [P, 1])
        vals = sb("vals", [P, 3])
        offs_i = sb("offs_i", [P, 2, NT], I32)
        rowoff, woff = offs_i[:, 0, :], offs_i[:, 1, :]
        skip = sb("skip", [P, NT])

        we = [sb(f"we{i}", [P, HID + NHALF * C]) for i in range(WB)]
        xs = [sb(f"xs{i}", [P, RW]) for i in range(XB)]
        xT = [sb(f"xT{i}", [P, TS]) for i in range(2)]
        hT = [sb(f"hT{i}", [P, NHALF, TS]) for i in range(2)]
        y_sb = [sb(f"y_sb{i}", [P, C]) for i in range(XB)]
        ret = [sb(f"ret{i}", [P, 1], U32) for i in range(XB)]
        gate = [sb(f"gate{i}", [P, 1]) for i in range(XB)]

        NY = TOK // P
        FB = 4
        YB = [(m, min(m + FB, NY)) for m in range(0, NY, FB)]
        yk = sb("yk", [P, TOPK, NY * C])
        ysum = sb("ysum", [P, NY * C])
        fin = x_sb

        ps = ctx.enter_context(nc.psum_tensor("ps", [P, 8 * 512], F32))

        def bank(i, n=512, p=P):
            return ps[0:p, i * 512:i * 512 + n]

        XC_Q, VAR_K, S0, AV0, V_B, PJ_B, TR_B, POS_B = 0, 1, 2, 4, 4, 5, 6, 7
        TL = ps[0:GT, TR_B * 512:TR_B * 512 + NG * (C + E)]
        POS = ps[0:GT, POS_B * 512:POS_B * 512 + NG * E]
        CNT = ps[0:P, POS_B * 512 + 64:POS_B * 512 + 64 + E]
        TAB = ps[0:P, POS_B * 512 + 128:POS_B * 512 + 128 + 3 * NT]
        s_view = ps[:, S0 * 512:(S0 + 2) * 512].rearrange("p (f n) -> p f n", f=HF)[:, :, 0:NG * HQ * W] \
            .rearrange("p f (a j) -> p f a j", j=W)
        av_view = ps[:, AV0 * 512:(AV0 + 4) * 512].rearrange("p (r n) -> p r n", r=RG)[:, :, 0:2 * NG * W] \
            .rearrange("p r (a n) -> p r a n", a=2)

        s_cst = sem("s_cst")
        s_cstv = sem("s_cstv")
        s_free = sem("s_free")
        s_carrier = sem("s_carrier")
        s_masks = sem("s_masks")
        s_xin = [sem(f"s_xin{i}") for i in range(2)]
        s_win = sem("s_win")
        s_wl = sem("s_wl")
        s_pre = sem("s_pre")
        s_wtp = sem("s_wtp")
        s_wt = sem("s_wt")
        s_v = sem("s_v")
        s_xc = sem("s_xc")
        s_sq = sem("s_sq")
        s_var = sem("s_var")
        s_xn = sem("s_xn")
        s_qp = sem("s_qp")
        s_kp = sem("s_kp")
        s_q = sem("s_q")
        s_km = sem("s_km")
        s_vp = sem("s_vp")
        s_vs = sem("s_vs")
        s_s = sem("s_s")
        s_sub = sem("s_sub")
        s_e = sem("s_e")
        s_et = sem("s_et")
        s_av = sem("s_av")
        s_av0 = sem("s_av0")
        s_o = sem("s_o")
        s_pj = sem("s_pj")
        s_t = sem("s_t")
        s_tcp = sem("s_tcp")
        s_lg = sem("s_lg")
        s_tl = sem("s_tl")
        s_st = sem("s_st")
        s_rows = sem("s_rows")
        s_rows2 = sem("s_rows2")
        s_m0 = sem("s_m0")
        s_mt = sem("s_mt")
        s_gx = sem("s_gx")
        s_pos = sem("s_pos")
        s_pb = sem("s_pb")
        s_macc = sem("s_macc")
        s_meta = sem("s_meta")
        s_scat = [sem(f"s_scat{i}") for i in range(2)]
        s_cnt = sem("s_cnt")
        s_facts = sem("s_facts")
        s_tabp = sem("s_tabp")
        s_tab = sem("s_tab")
        s_ld = [sem(f"s_ld{i}") for i in range(XB)]
        s_trx = sem("s_trx")
        s_xT = sem("s_xT")
        s_h = sem("s_h")
        s_g = sem("s_g")
        s_we = sem("s_we")
        s_yp = sem("s_yp")
        s_y = sem("s_y")
        s_ret = sem("s_ret")
        s_ysc = [sem(f"s_ysc{i}") for i in range(XB)]
        s_yk = [sem(f"s_yk{i}") for i in range(len(YB))]
        s_ys = sem("s_ys")
        s_yt = sem("s_yt")
        s_fin = sem("s_fin")
        s_out = sem("s_out")

        s_rs, s_mx, s_den, s_rden, s_nrm, s_bst, s_bmv, s_rs2, s_lgs, s_m8, s_i8, s_idx, s_oh, s_ms, s_ma, \
            s_pr, s_df, s_rg, s_ids, s_lnv, s_lnv2 = [sem(f"s_{k}") for k in (
                "rs", "mx", "den", "rden", "nrm", "bst", "bmv", "rs2", "lgs", "m8", "i8", "idx", "oh", "ms",
                "ma", "pr", "df", "rg", "ids", "lnv", "lnv2")]

        NCST = 12
        CREDIT = 1
        TPI = 2

        def has(k):
            return not isinstance(k, int) or 0 <= k < NCH

        def steps(eng, step):
            for n in range(-3, 1):
                step(n, n % 2)
            with eng.Fori(0, (NCH - 4) // 2) as i:
                for j in (1, 2):
                    step(i * 2 + j, j % 2)
            for n in range(NCH - 3, NCH + 1):
                step(n, n % 2)

        def tiles(eng, step, last=NT):
            for j in range(HEAD):
                step(0, j)
            with eng.Fori(0, LOOPS) as i:
                for j in range(HEAD, HEAD + XB):
                    step(i, j)
            for t in range(HEAD + LOOPS * XB, last):
                step(0, t)

        def used(i, j):
            return i * 16 + 16 * (j // XB + 1)


        block = ctx.enter_context(nc.Block())

        @block.sync
        def _(sp):
            sp.dma_start(wqkv_sb[:, :, :], w_qkv.rearrange("(a o) c -> o a c", a=3)).then_inc(s_win, 16)
            sp.dma_start(x_sb[:, 0:TOK // B], x_v[:, 0, :]).then_inc(s_xin[0], 16)
            sp.dma_start(x_sb[:, TOK // B:].rearrange("c (b n) -> c b n", b=B - 1),
                         x_v[:, 1:, :]).then_inc(s_xin[1], 16)
            sp.wait_ge(s_cstv, 2)
            sp.dma_start(slots.rearrange("(e p) w -> p e w", e=E)[0:TS, :, :],
                         pad_rows[:, :].unsqueeze(1).broadcast_to([P, E, RW])).then_inc(s_pre, 16)
            sp.wait_ge(s_xin[1], 16)
            sp.dma_start(w_sb[:, :, 0:HID], w1.rearrange("e d h -> d e h")).then_inc(s_wl, 16)
            for f in range(NHALF):
                sp.dma_start(w_sb[:, :, HID + f * C:HID + (f + 1) * C],
                             w2[:, f * P:(f + 1) * P, :].rearrange("e p d -> p e d")).then_inc(s_wl, 16)
            sp.sem_inc(s_free, TPI)
            with sp.Fori(0, NCH // TPI) as i:
                for c in range(TPI):
                    sp.wait_ge(s_scat[c], i * (16 * TOPK * NG) + 16 * TOPK * NG)
                    sp.sem_inc(s_free, 1)
            sp.wait_ge(s_tab, 1)
            sp.wait_ge(s_pre, 16)
            sp.wait_ge(s_scat[0], 16 * TOPK * NG * NCH // 2)
            sp.wait_ge(s_scat[1], 16 * TOPK * NG * NCH // 2)
            def load(off, i, j):
                sp.dma_start(xs[j % XB][:, :], slots[bass.DynSlice(off, TS), :]).then_inc(s_ld[j % XB], 16)

            def offsets(t, n):
                return nc.values_load_multi_w_load_instructions(
                    rowoff[0:1, bass.ds(t, n)], engines=(sp.engine,), min_val=0, max_val=E * CAP - TS,
                    skip_runtime_bounds_check_because=IN_RANGE)[1]

            for j0 in range(0, XB, 4):
                for j, off in enumerate(offsets(j0, 4)):
                    load(off, 0, j0 + j)

            def reload(i, j, off):
                t = i * XB + j
                sp.wait_ge(s_trx, t + 1)
                sp.wait_ge(s_ret, t + 1)
                load(off, i, j)

            for j, off in enumerate(offsets(XB, HEAD)):
                reload(0, j, off)
            with sp.Fori(0, LOOPS) as i:
                for j0 in range(HEAD, HEAD + XB, 4):
                    for j, off in enumerate(offsets(i * XB + j0 + XB, 4)):
                        reload(i, j0 + j, off)
            for b in range(XB):
                sp.wait_ge(s_ysc[b], 16 * len(range(b, NT, XB)))
            y_v = y_rows.rearrange("(k n p) d -> p k n d", k=TOPK, p=P)
            for b, (n0, n1) in enumerate(YB):
                for k in range(TOPK):
                    sp.dma_start(yk[:, k, n0 * C:n1 * C].rearrange("p (n d) -> p n d", d=C),
                                 y_v[:, k, n0:n1, :]).then_inc(s_yk[b], 16)
            for b in range(B):
                sp.wait_ge(s_fin, -(-(b + 1) * (TOK // B) // (FB * P)))
                sp.dma_start(out_v[:, b, :], fin[:, b * (TOK // B):(b + 1) * (TOK // B)]).then_inc(s_out, 16)
            sp.wait_ge(s_out, 16 * B)

        @block.gpsimd
        def _(pool):
            g = nc.gpsimd
            for free in (s_ids, s_tcp):
                pool.sem_inc(free, CREDIT)
            g.memset(chunk_step[:, :, :], float(CT))
            g.memset(ident[:, :], 0.0).then_inc(s_cst, 1)
            g.memset(tri[:, :], 0.0).then_inc(s_cst, 1)
            g.memset(hmask[:, :], 1.0).then_inc(s_cst, 1)
            pool.wait_ge(s_cst, 3)
            g.affine_select(out=ident[:, :], in_=ident[:, :], compare_op=ALU.not_equal, fill=1.0,
                            base=0, pattern=[[-1, P]], channel_multiplier=1).then_inc(s_cst, 1)
            g.affine_select(out=tri[:, :], in_=tri[:, :], compare_op=ALU.is_ge, fill=1.0,
                            base=0, pattern=[[-1, GT]], channel_multiplier=1).then_inc(s_cst, 1)
            g.affine_select(out=hmask[:, :], in_=hmask[:, :], compare_op=ALU.is_ge, fill=0.0,
                            base=0, pattern=[[-HD, HEADS]], channel_multiplier=1).then_inc(s_cst, 1)
            pool.wait_ge(s_cst, 6)
            g.affine_select(out=hmask[:, :], in_=hmask[:, :], compare_op=ALU.is_ge, fill=0.0,
                            base=HD - 1, pattern=[[HD, HEADS]], channel_multiplier=-1).then_inc(s_cst, 1)
            exact = dict(allow_small_or_imprecise_dtypes=True)
            g.iota(iota_e[:, :], pattern=[[1, E]], base=0, channel_multiplier=0, **exact).then_inc(s_cst, 1)
            g.iota(ebase[:, :], pattern=[[CAP, E]], base=0, channel_multiplier=0, **exact).then_inc(s_cst, 1)
            g.iota(ids[:, :, :], pattern=[[TOK, TOPK], [GT, NG]], base=0, channel_multiplier=1,
                   **exact).then_inc(s_cst, 1)
            g.iota(iota_s[:, :], pattern=[[0, 1]], base=0, channel_multiplier=TS, **exact).then_inc(s_cst, 1)
            g.iota(iota_p[:, :], pattern=[[0, 1]], base=0, channel_multiplier=1, **exact).then_inc(s_cst, 1)
            pool.wait_ge(s_pre, 16)
            def step(n, c):
                if has(n):
                    pool.wait_ge(s_t, n + 1)
                    pool.sem_inc(s_carrier, 1)
                    g.tensor_copy(t_sb[:, bass.ds(n * CT, CT)], tc[c][:, :]).then_inc(s_tcp, 1)
                m, o = n - 1, 1 - c
                if has(m):
                    pool.wait_ge(s_rows, m + 1)
                    pool.sem_inc(s_carrier, 1)
                    g.tensor_copy(rows[o][:, 1, :, 0:C], rows[o][:, 0, :, 0:C]).then_inc(s_rows2, 1)
                    pool.wait_ge(s_rows2, m + 1)
                    pool.wait_ge(s_meta, m + 1)
                    g.tensor_tensor(ids[:, :, :], ids[:, :, :], chunk_step[:, :, :], ALU.add).then_inc(s_ids, 1)
                    for k in range(TOPK):
                        for gr in range(NG):
                            g.indirect_dma_start(
                                out=slots[:, :],
                                out_offset=bass.IndirectOffsetOnAxis(
                                    ap=dest[o][:, k * NG + gr:k * NG + gr + 1], axis=0),
                                in_=rows[o][:, k, gr, :], in_offset=None).then_inc(s_scat[o], 16)

            steps(pool, step)
            def scatter_outputs(i, j):
                b = j % XB
                pool.wait_ge(s_y, i * XB + j + 1)
                pool.sem_inc(s_carrier, 1)
                g.indirect_dma_start(
                    out=y_rows[:, :], out_offset=bass.IndirectOffsetOnAxis(ap=ret[b][:, 0:1], axis=0),
                    in_=y_sb[b][:, :], in_offset=None,
                    bounds_check=YROWS - 1, oob_is_err=False).then_inc(s_ysc[b], 16)

            tiles(pool, scatter_outputs)

        @block.scalar
        def _(act):
            a = nc.scalar
            act.dma_start(wout_sb[:, :], w_out).then_inc(s_win, 16)
            act.dma_start(wg[:, :], w_gate).then_inc(s_win, 16)
            act.dma_start(bo[:, :], b_out.rearrange("(c a) -> c a", a=1)).then_inc(s_win, 16)
            act.preload_act_table_set("natural_log_exp_and_others")
            act.wait_ge(s_cst, NCST)
            act.wait_ge(s_wtp, 1)
            a.activation(wT[:, :, :], bank(1).rearrange("p (a c) -> p a c", a=4), ACT.Copy).then_inc(s_wt, 1)
            act.wait_ge(s_wtp, 2)
            a.activation(wgc[:, :], bank(0, E), ACT.Copy).then_inc(s_wt, 1)

            def squares(k, c):
                act.wait_ge(s_xc, k + 1)
                a.activation(sq[c][:, :], bank(XC_Q, CT), ACT.Square).then_inc(s_sq, 1)

            def channel_rstd(k):
                act.wait_ge(s_var, k + 1)
                if not isinstance(k, int) or k > 0:
                    act.wait_ge(s_xn, k)
                a.activation(lnv[:, :], bank(VAR_K, CT), ACT.Ln, bias=eps_c[:, 0:1]).then_inc(s_lnv, 1)
                act.wait_ge(s_lnv, k + 1)
                a.activation(rstd[:, :], lnv[:, :], ACT.Exp, scale=-0.5).then_inc(s_rs, 1)

            def queries(k, c):
                act.wait_ge(s_qp, k + 1)
                a.activation(qs[c][:, :].rearrange("p (a w) -> p a w", w=WP)[:, :, 0:W],
                             bank(XC_Q, CT).rearrange("p (a w) -> p a w", w=W), ACT.Copy).then_inc(s_q, 1)

            def masked_keys(k, c):
                act.wait_ge(s_kp, k + 1)
                for hq in range(HQ):
                    last = a.activation(km[c][:, hq, :], bank(VAR_K, CT), ACT.Identity,
                                        bias=zero_c[:, 0:1], scale=kmask[:, hq:hq + 1])
                last.then_inc(s_km, 1)

            def values(k, c):
                act.wait_ge(s_vp, k + 1)
                a.activation(vs[c][:, :], bank(V_B, NG * C), ACT.Copy).then_inc(s_vs, 1)

            def exps(k, c):
                act.wait_ge(s_sub, k + 1)
                a.activation(ex[c][:, :, 0:W], es[c][:, :, :], ACT.Exp).then_inc(s_e, 1)

            def first_heads(n, c):
                act.wait_ge(s_av, n + 1)
                a.activation(av0[:, :].rearrange("p (r n) -> p r n", r=RG), av_view[:, :, 0, :], ACT.Identity,
                             bias=zero_c[:, 0:1], scale=pmask[:, 0:1]).then_inc(s_av0, 1)

            def token_rows(n):
                act.wait_ge(s_lg, n + 1)
                a.activation(tl_sb[:, :], TL, ACT.Copy).then_inc(s_tl, 1)

            def token_rstd(m):
                act.wait_ge(s_bmv, m + 1)
                a.activation(lnv2[:, :], bmv[:, :, 1], ACT.Ln, bias=eps_t[0:GT, 0:1]).then_inc(s_lnv2, 1)
                act.wait_ge(s_lnv2, m + 1)
                a.activation(rstd2[:, :], lnv2[:, :], ACT.Exp, scale=-0.5).then_inc(s_rs2, 1)

            def normed_rows(m, c):
                act.wait_ge(s_st, m + 1)
                act.wait_ge(s_free, m + 1)
                for gr in range(NG):
                    last = a.activation(rows[c][:, 0, gr, 0:C], tl_sb[:, gr * (C + E):gr * (C + E) + C],
                                        ACT.Identity, bias=nmr[:, gr:gr + 1], scale=rstd2[:, gr:gr + 1])
                last.then_inc(s_rows, 1)

            def gate_exps(m):
                act.wait_ge(s_m0, m + 1)
                for gr in range(NG):
                    a.activation(junk[:, gr, :], lg[:, gr, :], ACT.Exp, bias=nm0[:, gr:gr + 1],
                                 accum_out=esum[:, gr:gr + 1])
                a.activation(e2[:, :], dm[:, :], ACT.Exp).then_inc(s_gx, 1)

            def step(n, c):
                o = 1 - c
                if has(n + 3):
                    squares(n + 3, o)
                if has(n - 1):
                    token_rstd(n - 1)
                if has(n + 3):
                    channel_rstd(n + 3)
                if has(n - 1):
                    normed_rows(n - 1, o)
                if has(n + 1):
                    exps(n + 1, o)
                if has(n):
                    first_heads(n, c)
                if has(n + 3):
                    queries(n + 3, o)
                    masked_keys(n + 3, o)
                if has(n + 2):
                    values(n + 2, c)
                if has(n):
                    token_rows(n)
                if has(n - 1):
                    gate_exps(n - 1)

            act.wait_ge(s_cstv, 2)
            steps(act, step)

            def take_xT(i, j):
                act.wait_ge(s_trx, i * XB + j + 1)
                a.activation(xT[j % 2][:, :], bank(j % 2, TS), ACT.Copy).then_inc(s_xT, 1)

            def gelu(i, j):
                act.wait_ge(s_h, i * XB + j + 1)
                a.activation(hT[j % 2][:, :, :].rearrange("p f s -> p (f s)"), bank(2 + j % 2, HID),
                             ACT.Gelu).then_inc(s_g, 1)

            def tile(i, j):
                last = isinstance(i, int)
                if not last or j + 2 < NT:
                    take_xT(i, j + 2)
                if not last or j + 1 < NT:
                    gelu(i, j + 1)

            take_xT(0, 0)
            take_xT(0, 1)
            gelu(0, 0)
            tiles(act, tile)

        @block.vector
        def _(dve):
            v = nc.vector
            for free in (s_pb, s_macc):
                dve.sem_inc(free, CREDIT)
            v.memset(zero_c[:, :], 0.0)
            v.memset(eps_c[:, :], EPS_C)
            v.memset(eps_t[:, :], EPS_T)
            v.memset(zeros[:, :], 0.0)
            v.memset(pad_rows[:, :], 0.0).then_inc(s_cstv, 1)
            dve.wait_ge(s_cstv, 1)
            v.memset(pad_rows[:, ID:ID + 1].bitcast(I32), SKIP)
            v.memset(avg[:, :], 1.0 / C)
            dve.wait_ge(s_cst, 7)
            for f in range(HF):
                v.tensor_scalar(hscale[:, f, :], hmask[:, f * HQ:(f + 1) * HQ], SCALE, None,
                                ALU.mult).then_inc(s_masks, 1)
            v.tensor_reduce(pmask[:, :], hmask[:, :].rearrange("c (p a) -> c a p", a=2), AX.X,
                            ALU.add).then_inc(s_masks, 1)
            dve.wait_ge(s_masks, 3)
            v.tensor_tensor(kmask[:, :], hscale[:, 0, :], hscale[:, 1, :], ALU.add)
            v.tensor_scalar(cmat[:, :], ident[:, :], -1.0 / C, None, ALU.add).then_inc(s_cstv, 1)
            v.memset(ones[:, :], 1.0)
            v.memset(one_e[:, :], 1.0)
            v.memset(macc[:, :], 0.0)
            v.memset(maccb[:, :], 0.0)
            v.memset(facts[:, :, 0:1], 0.0)
            for c in range(2):
                v.memset(xn[c][:, :].rearrange("p (a w) -> p a w", w=WP)[:, :, W:], 0.0)
                v.memset(qs[c][:, :].rearrange("p (a w) -> p a w", w=WP)[:, :, W:], 0.0)
                v.memset(ex[c][:, :, W:], 0.0)
                v.memset(rows[c][:, :, :, C:], 0.0)
            dve.wait_ge(s_cst, NCST)

            def layer_norm(k, c):
                dve.wait_ge(s_rs, k + 1)
                v.tensor_tensor(xn[c][:, :].rearrange("p (a w) -> p a w", w=WP)[:, :, 0:W],
                                bank(XC_Q, CT).rearrange("p (a w) -> p a w", w=W),
                                rstd[:, :].rearrange("p (a w) -> p a w", w=W), ALU.mult).then_inc(s_xn, 1)

            NS = HF * NG * HQ

            def row_max(k, c):
                dve.wait_ge(s_s, k + 1)
                v.tensor_reduce(mx[:, :].rearrange("p (f a) -> p f a", f=HF), s_view, AX.X,
                                ALU.max).then_inc(s_mx, 1)
                dve.wait_ge(s_mx, k + 1)
                v.tensor_tensor(es[c][:, :, :].rearrange("p (f a) j -> p f a j", f=HF), s_view,
                                mx[:, :].rearrange("p (f a) -> p f a", f=HF).unsqueeze(3)
                                .broadcast_to([P, HF, NG * HQ, W]), ALU.subtract).then_inc(s_sub, 1)

            def row_sum(k, c):
                dve.wait_ge(s_e, k + 1)
                v.tensor_reduce(den[:, :], ex[c][:, :, 0:W], AX.X, ALU.add).then_inc(s_den, 1)
                dve.wait_ge(s_den, k + 1)
                v.reciprocal(rden[:, :], den[:, :]).then_inc(s_rden, 1)

            def normalise(k, c):
                dve.wait_ge(s_rden, k + 1)
                v.tensor_tensor(ex[c][:, :, 0:W], ex[c][:, :, 0:W],
                                rden[:, :].unsqueeze(2).broadcast_to([P, NS, W]), ALU.mult).then_inc(s_nrm, 1)

            def turn(k, c):
                dve.wait_ge(s_nrm, k + 1)
                v.transpose(exT[c][:, :, :].rearrange("p a w -> p (a w)"),
                            ex[c][:, :, :].rearrange("p a w -> p (a w)")).then_inc(s_et, 1)

            def attn_out(n, c):
                dve.wait_ge(s_av0, n + 1)
                v.scalar_tensor_tensor(o_sb[c][:, :].rearrange("p (r n) -> p r n", r=RG), av_view[:, :, 1, :],
                                       pmask[:, 1:2], av0[:, :].rearrange("p (r n) -> p r n", r=RG),
                                       ALU.mult, ALU.add).then_inc(s_o, 1)

            def residual(n, c):
                dve.wait_ge(s_pj, n + 1)
                if not isinstance(n, int) or n >= 2:
                    dve.wait_ge(s_tcp, n - 1 + CREDIT)
                v.scalar_tensor_tensor(tc[c][:, :], bank(PJ_B, CT), bo[:, 0:1], x_sb[:, bass.ds(n * CT, CT)],
                                       ALU.add, ALU.add).then_inc(s_t, 1)

            def token_stats(m):
                dve.wait_ge(s_tl, m + 1)
                for gr in range(NG):
                    last = v.bn_stats(bst[:, gr, :], tl_sb[:, gr * (C + E):gr * (C + E) + C])
                last.then_inc(s_bst, 1)
                dve.wait_ge(s_win, 64)
                dve.wait_ge(s_bst, m + 1)
                for gr in range(NG):
                    last = v.bn_aggr(bmv[:, gr, :], bst[:, gr, :])
                last.then_inc(s_bmv, 1)

            def mean_term(m):
                dve.wait_ge(s_bmv, m + 1)
                dve.wait_ge(s_rs2, m + 1)
                v.scalar_tensor_tensor(nmr[:, :], bmv[:, :, 0], -1.0, rstd2[:, :], ALU.mult,
                                       ALU.mult).then_inc(s_st, 1)

            def logits(m):
                v.tensor_tensor(lg[:, :, :], tl_sb[:, :].rearrange("p (g e) -> p g e", g=NG)[:, :, C:],
                                rstd2[:, :].unsqueeze(2).broadcast_to([GT, NG, E]), ALU.mult).then_inc(s_lgs, 1)

            def top2(m):
                dve.wait_ge(s_win, 64)
                dve.wait_ge(s_lgs, m + 1)
                for gr in range(NG):
                    last = v.max(m8[:, gr, :], lg[:, gr, :])
                last.then_inc(s_m8, 1)
                dve.wait_ge(s_win, 64)
                dve.wait_ge(s_m8, m + 1)
                for gr in range(NG):
                    last = v.max_index(i8[:, gr, :], m8[:, gr, :], lg[:, gr, :])
                last.then_inc(s_i8, 1)
                v.tensor_tensor(dm[:, :], m8[:, :, 1], m8[:, :, 0], ALU.subtract)
                v.tensor_scalar(nm0[:, :], m8[:, :, 0], -1.0, None, ALU.mult).then_inc(s_m0, 1)
                dve.wait_ge(s_i8, m + 1)
                v.tensor_copy(idx[:, :, :], i8[:, :, 0:TOPK].rearrange("p g k -> p k g")).then_inc(s_idx, 1)
                dve.wait_ge(s_idx, m + 1)
                v.tensor_tensor(oh[:, :, :].rearrange("p k (g e) -> p (k g) e", e=E),
                                iota_e[0:GT, :].unsqueeze(1).broadcast_to([GT, TOPK * NG, E]),
                                idx[:, :, :].rearrange("p k g -> p (k g)").unsqueeze(2)
                                .broadcast_to([GT, TOPK * NG, E]), ALU.is_equal).then_inc(s_oh, 1)
                dve.wait_ge(s_oh, m + 1)
                v.tensor_tensor(mt[:, :, :].rearrange("p g e -> p (g e)"), oh[:, 0, :], oh[:, 1, :],
                                ALU.add).then_inc(s_mt, 1)

            def slot_rows(m, c):
                dve.wait_ge(s_mt, m + 1)
                v.tensor_reduce(msum[:, :], mt[:, :, :].rearrange("p g e -> p e g"), AX.X,
                                ALU.add).then_inc(s_ms, 1)
                dve.wait_ge(s_pos, m + 1)
                v.tensor_tensor(posb[:, :].rearrange("p (g e) -> p g e", g=NG),
                                POS.rearrange("p (g e) -> p g e", g=NG),
                                ebase[0:GT, :].unsqueeze(1).broadcast_to([GT, NG, E]), ALU.add).then_inc(s_pb, 1)
                dve.wait_ge(s_ms, m + 1)
                v.tensor_tensor(macc[:, :], macc[:, :], msum[:, :], ALU.add).then_inc(s_ma, 1)
                dve.wait_ge(s_pb, m + 1 + CREDIT)
                v.tensor_tensor(prod[:, :, :], oh[:, :, :], posb[:, :].unsqueeze(1)
                                .broadcast_to([GT, TOPK, NG * E]), ALU.mult).then_inc(s_pr, 1)
                dve.wait_ge(s_ma, m + 1)
                v.tensor_copy(maccb[:, :], macc[:, :]).then_inc(s_macc, 1)
                dve.wait_ge(s_pr, m + 1)
                v.tensor_reduce(destf[:, :], prod[:, :, :].rearrange("p k (g e) -> p (k g) e", e=E), AX.X,
                                ALU.add).then_inc(s_df, 1)
                dve.wait_ge(s_gx, m + 1)
                v.reciprocal(rg[:, :], esum[:, :]).then_inc(s_rg, 1)
                dve.wait_ge(s_free, m + 1)
                dve.wait_ge(s_df, m + 1)
                v.tensor_copy(dest[c][:, :], destf[:, :])
                dve.wait_ge(s_ids, m + CREDIT)
                v.tensor_copy(rows[c][:, :, :, ID].bitcast(U32), ids[:, :, :])
                dve.wait_ge(s_rg, m + 1)
                v.tensor_copy(rows[c][:, 0, :, GATE], rg[:, :])
                v.tensor_tensor(rows[c][:, 1, :, GATE], rg[:, :], e2[:, :], ALU.mult).then_inc(s_meta, 1)

            def step(n, c):
                o = 1 - c
                if has(n - 1):
                    token_stats(n - 1)
                    mean_term(n - 1)
                    logits(n - 1)
                if has(n + 1):
                    row_max(n + 1, o)
                if has(n + 3):
                    layer_norm(n + 3, o)
                if has(n + 1):
                    row_sum(n + 1, o)
                if has(n):
                    attn_out(n, c)
                if has(n + 1):
                    normalise(n + 1, o)
                if has(n):
                    residual(n, c)
                if has(n - 1):
                    top2(n - 1)
                if has(n + 1):
                    turn(n + 1, o)
                if has(n - 1):
                    slot_rows(n - 1, o)

            dve.wait_ge(s_win, 64)
            steps(dve, step)

            step_no = [0]

            def then(*steps_of_one_level):
                for ins in steps_of_one_level:
                    ins.then_inc(s_v, 1)
                    step_no[0] += 1
                dve.wait_ge(s_v, step_no[0])

            dve.wait_ge(s_cnt, 1)
            then(v.tensor_copy(cnt[:, :], CNT),
                 v.tensor_scalar(nt_i[:, :], CNT, float(TS - 1), None, ALU.add))
            then(v.tensor_scalar(nt_i[:, :], nt_i[:, :], TS.bit_length() - 1, None, ALU.logical_shift_right))
            then(v.tensor_copy(nt_f[:, :], nt_i[:, :]))
            then(v.tensor_tensor_scan(ct_f[:, :], one_e[:, :], nt_f[:, :], 0.0, ALU.mult, ALU.add))
            past = facts[:, 0, 1:]
            then(v.tensor_scalar(past, ct_f[:, :], iota_p[:, 0:1], None, ALU.is_le))
            then(v.tensor_tensor(facts[:, 1, 1:], past, nt_f[:, :], ALU.mult),
                 v.tensor_tensor(mine[:, 1:], past[:, 0:E - 1], past[:, 1:], ALU.subtract),
                 v.tensor_scalar(mine[:, 0:1], past[:, 0:1], -1.0, 1.0, ALU.mult, ALU.add))
            then(v.tensor_tensor(facts[:, 2, 1:], mine[:, :], cnt[:, :], ALU.mult))
            then(v.tensor_reduce(sums3[:, :], facts[:, :, :], AX.X, ALU.add))
            expert, first, count = (sums3[:, k:k + 1] for k in range(3))
            then(v.scalar_tensor_tensor(list_row[:, :], first, -float(TS), iota_s[:, :], ALU.mult, ALU.add),
                 v.tensor_scalar(e_c[:, :], expert, float(E - 1), None, ALU.min),
                 v.tensor_scalar(none[:, :], expert, float(E), float(TS), ALU.is_equal, ALU.mult))
            then(v.scalar_tensor_tensor(start[:, :], count, -float(TS), list_row[:, :], ALU.add, ALU.min))
            then(v.tensor_scalar(start[:, :], start[:, :], 0.0, None, ALU.max))
            v.scalar_tensor_tensor(vals[:, 0:1], e_c[:, :], float(CAP), start[:, :], ALU.mult, ALU.add)
            v.tensor_scalar(vals[:, 1:2], e_c[:, :], float(HID + NHALF * C), None, ALU.mult)
            v.tensor_scalar(vals[:, 2:3], list_row[:, :], start[:, 0:1], none[:, 0:1], ALU.subtract,
                            ALU.add).then_inc(s_facts, 1)
            dve.wait_ge(s_tabp, 1)
            v.tensor_copy(offs_i[:, :, :].rearrange("p a t -> p (a t)"), TAB[:, 0:2 * NT]).then_inc(s_tab, 1)
            v.tensor_scalar(skip[:, :], TAB[:, 2 * NT:], iota_p[:, 0:1], float(SKIP), ALU.is_gt,
                            ALU.mult).then_inc(s_tab, 1)
            dve.wait_ge(s_tab, 2)

            def ahead(off, i, j):
                b = j % XB
                dve.wait_ge(s_ld[b], used(i, j))
                if j >= XB:
                    dve.wait_ge(s_ysc[b], used(i, j - XB))
                elif not isinstance(i, int):
                    dve.wait_ge(s_ysc[b], i * 16)
                v.tensor_copy(gate[b][:, :], xs[b][:, GATE:GATE + 1])
                v.tensor_tensor(ret[b][:, :], xs[b][:, ID:ID + 1].bitcast(U32), skip[:, bass.ds(i * XB + j, 1)],
                                ALU.add).then_inc(s_ret, 1)
                v.tensor_copy(we[j % WB][:, :], w_flat[:, bass.ds(off, HID + NHALF * C)]).then_inc(s_we, 1)

            def expert_offsets(t, n):
                return nc.values_load_multi_w_load_instructions(
                    woff[0:1, bass.ds(t, n)], engines=(dve.engine,), min_val=0,
                    max_val=(E - 1) * (HID + NHALF * C), skip_runtime_bounds_check_because=IN_RANGE)[1]

            def tile(i, j, off):
                b = j % XB
                if off is not None:
                    ahead(off, i, j + 2)
                dve.wait_ge(s_yp, i * XB + j + 1)
                v.tensor_scalar(y_sb[b][:, :], bank(6 + j % 2, C), gate[b][:, :], None,
                                ALU.mult).then_inc(s_y, 1)

            dve.wait_ge(s_wl, 16 * (1 + NHALF))
            w_flat = w_sb[:, :, :].rearrange("p e n -> p (e n)")
            offs = expert_offsets(0, HEAD + 2)
            ahead(offs[0], 0, 0)
            ahead(offs[1], 0, 1)
            for j in range(HEAD):
                tile(0, j, offs[j + 2])
            with dve.Fori(0, LOOPS) as i:
                for j0 in range(HEAD, HEAD + XB, 4):
                    for j, off in enumerate(expert_offsets(i * XB + j0 + 2, 4)):
                        tile(i, j0 + j, off)
            t0 = HEAD + LOOPS * XB
            for j0 in range(t0, NT, 4):
                offs = expert_offsets(j0 + 2, min(4, NT - j0 - 2))
                for j in range(4):
                    tile(0, j0 + j, offs[j] if j < len(offs) else None)

            for b, (n0, n1) in enumerate(YB):
                dve.wait_ge(s_yk[b], 16 * TOPK)
                v.tensor_tensor(ysum[:, n0 * C:n1 * C], yk[:, 0, n0 * C:n1 * C], yk[:, 1, n0 * C:n1 * C],
                                ALU.add).then_inc(s_ys, 1)
            for b, (n0, n1) in enumerate(YB):
                dve.wait_ge(s_yt, b + 1)
                v.tensor_tensor(fin[:, n0 * P:n1 * P], ps[:, n0 * P:n1 * P], t_sb[:, n0 * P:n1 * P],
                                ALU.add).then_inc(s_fin, 1)

        @block.tensor
        def _(pe):
            mm = nc.tensor.matmul
            pe.wait_ge(s_cstv, 1)
            for _ in range(WARM):
                mm(bank(7), zeros[:, 0:P], zeros[:, :], start=True, stop=True)
            pe.wait_ge(s_cst, NCST)
            pe.wait_ge(s_win, 64)
            for k in range(3):
                nc.tensor.transpose(ps[:, 512 + k * C:512 + (k + 1) * C], wqkv_sb[:, k, :], ident[:, :])
            nc.tensor.transpose(ps[:, 512 + 3 * C:512 + 4 * C], wout_sb[:, :], ident[:, :]).then_inc(s_wtp, 1)
            pe.wait_ge(s_cstv, 2)
            mm(bank(0, E), cmat[:, :], wg[:, :], start=True, stop=True).then_inc(s_wtp, 1)
            pe.wait_ge(s_wt, 2)
            pe.wait_ge(s_xin[0], 16)

            def centre(k):
                if isinstance(k, int) and k == 2:
                    pe.wait_ge(s_xin[1], 16)
                if not isinstance(k, int) or k > 0:
                    pe.wait_ge(s_q, k)
                mm(bank(XC_Q, CT), cmat[:, :], x_sb[:, bass.ds(k * CT, CT)], start=True,
                   stop=True).then_inc(s_xc, 1)

            def variance(k, c):
                pe.wait_ge(s_sq, k + 1)
                if not isinstance(k, int) or k > 0:
                    pe.wait_ge(s_km, k)
                mm(bank(VAR_K, CT), avg[:, :], sq[c][:, :], start=True, stop=True).then_inc(s_var, 1)

            def query_proj(k, c):
                pe.wait_ge(s_xn, k + 1)
                mm(bank(XC_Q, CT), wT[:, 0, :], xn[c][:, :].rearrange("p (a w) -> p a w", w=WP)[:, :, 0:W],
                   start=True, stop=True).then_inc(s_qp, 1)

            def key_proj(k, c):
                mm(bank(VAR_K, CT), wT[:, 1, :], xn[c][:, :].rearrange("p (a w) -> p a w", w=WP)[:, :, 0:W],
                   start=True, stop=True).then_inc(s_kp, 1)

            def value_rows(k, c):
                if isinstance(k, int) and k == 1:
                    pe.wait_ge(s_vs, 1)
                elif not isinstance(k, int) or k > 1:
                    pe.wait_ge(s_o, k - 1)
                for gr in range(NG):
                    last = mm(ps[:, V_B * 512 + gr * C:V_B * 512 + (gr + 1) * C], xn[c][:, gr * P:(gr + 1) * P],
                              wT[:, 2, :], start=True, stop=True)
                last.then_inc(s_vp, 1)

            def scores(k, c):
                if not isinstance(k, int) or k > 0:
                    pe.wait_ge(s_sub, k)
                pe.wait_ge(s_q, k + 1)
                pe.wait_ge(s_km, k + 1)
                pe.sem_inc(s_carrier, 1)
                for gr in range(NG):
                    for r in range(RG):
                        row = gr * RG + r
                        for f in range(HF):
                            col = (S0 + f) * 512 + gr * HQ * W
                            last = mm(ps[r * 32:(r + 1) * 32, col:col + HQ * W],
                                      qs[c][f * 64:(f + 1) * 64, row * WP:(row + 1) * WP],
                                      km[c][f * 64:(f + 1) * 64, :, row * W:(row + 1) * W],
                                      start=True, stop=True)
                last.then_inc(s_s, 1)

            def attend_ready(n):
                pe.wait_ge(s_vs, n + 2 if has(n + 1) else n + 1)
                if not isinstance(n, int) or n > 0:
                    pe.wait_ge(s_tl, n)
                    pe.wait_ge(s_pb, n - 1 + CREDIT)
                pe.wait_ge(s_et, n + 1)
                pe.sem_inc(s_carrier, 1)

            def attend(n, c, gr):
                for p in range(NP):
                    for r in range(RG):
                        a0 = (2 * p // HQ) * NG * HQ + gr * HQ + 2 * p % HQ
                        out_ap = av_view[p * 32:(p + 1) * 32, r, :, gr * W:(gr + 1) * W]
                        last = mm(out_ap, vs[c][r * 32:(r + 1) * 32, gr * C + p * 32:gr * C + (p + 1) * 32],
                                  exT[c][r * 32:(r + 1) * 32, a0:a0 + 2, 0:W], start=True, stop=True)
                if gr == NG - 1:
                    last.then_inc(s_av, 1)

            def out_proj(n, c):
                pe.wait_ge(s_o, n + 1)
                mm(bank(PJ_B, CT), wT[:, 3, :],
                   o_sb[c][:, :].rearrange("p (r g i) -> p g r i", r=RG, g=NG), start=True, stop=True).then_inc(s_pj, 1)

            def token_major(n, c):
                pe.wait_ge(s_t, n + 1)
                for gr in range(NG):
                    last = mm(TL[:, gr * (C + E):(gr + 1) * (C + E)], tc[c][:, gr * GT:(gr + 1) * GT],
                              id_wg[:, :], start=True, stop=True)
                last.then_inc(s_lg, 1)

            def places(m):
                pe.wait_ge(s_macc, m + CREDIT)
                pe.wait_ge(s_mt, m + 1)
                for gr in range(NG):
                    col = POS[:, gr * E:(gr + 1) * E]
                    mm(col, ones[:, 0:GT], maccb[:, :], start=True, stop=False)
                    for before in range(gr):
                        mm(col, ones[:, 0:GT], mt[:, before, :], start=False, stop=False)
                    last = mm(col, tri[:, :], mt[:, gr, :], start=False, stop=True)
                last.then_inc(s_pos, 1)

            def counts():
                pe.wait_ge(s_macc, NCH - 1 + CREDIT)
                pe.wait_ge(s_mt, NCH)
                mm(CNT, ones[:, :], maccb[:, :], start=True, stop=False)
                for gr in range(NG):
                    last = mm(CNT, ones[:, :], mt[:, gr, :], start=False, stop=gr == NG - 1)
                last.then_inc(s_cnt, 1)

            def step(n, c):
                o = 1 - c
                if has(n + 1):
                    scores(n + 1, o)
                if has(n + 3):
                    centre(n + 3)
                if has(n):
                    attend_ready(n)
                    attend(n, c, 0)
                if has(n + 3):
                    variance(n + 3, o)
                if has(n):
                    attend(n, c, 1)
                    attend(n, c, 2)
                if has(n + 3):
                    query_proj(n + 3, o)
                    key_proj(n + 3, o)
                if has(n):
                    out_proj(n, c)
                if has(n + 2):
                    value_rows(n + 2, c)
                if has(n):
                    token_major(n, c)
                if isinstance(n, int) and n == NCH:
                    counts()
                if has(n - 1):
                    places(n - 1)

            steps(pe, step)
            pe.wait_ge(s_facts, 1)
            for k in range(3):
                last = mm(TAB[:, k * NT:(k + 1) * NT], vals[0:NT, k:k + 1].broadcast_to([NT, P]),
                          ident[0:NT, 0:NT], start=True, stop=True)
            last.then_inc(s_tabp, 1)

            def rows_T(i, j):
                pe.wait_ge(s_ld[j % XB], used(i, j))
                nc.tensor.transpose(bank(j % 2, TS), xs[j % XB][:, 0:C], ident[:, :]).then_inc(s_trx, 1)

            def hidden(i, j):
                pe.wait_ge(s_we, i * XB + j + 1)
                pe.wait_ge(s_xT, i * XB + j + 1)
                for f in range(NHALF):
                    last = mm(ps[:, (2 + j % 2) * 512 + f * TS:(2 + j % 2) * 512 + (f + 1) * TS],
                              we[j % WB][:, f * P:(f + 1) * P], xT[j % 2][:, :], start=True, stop=True)
                last.then_inc(s_h, 1)

            def outputs(i, j):
                if isinstance(i, int) and j == NT - 1:
                    pe.wait_ge(s_y, NT - 2)
                pe.wait_ge(s_g, i * XB + j + 1)
                for f in range(NHALF):
                    last = mm(bank(6 + j % 2, C), hT[j % 2][:, f, :],
                              we[j % WB][:, HID + f * C:HID + (f + 1) * C], start=(f == 0), stop=(f == NHALF - 1))
                last.then_inc(s_yp, 1)

            def tile(i, j):
                last = isinstance(i, int)
                if not last or j + 2 < NT:
                    rows_T(i, j + 2)
                if not last or j + 1 < NT:
                    hidden(i, j + 1)
                outputs(i, j)

            rows_T(0, 0)
            rows_T(0, 1)
            hidden(0, 0)
            tiles(pe, tile)

            pe.wait_ge(s_y, NT)
            for b, (n0, n1) in enumerate(YB):
                pe.wait_ge(s_ys, b + 1)
                for m in range(n0, n1):
                    last = nc.tensor.transpose(ps[:, m * P:(m + 1) * P], ysum[:, m * C:(m + 1) * C], ident[:, :])
                last.then_inc(s_yt, 1)


_INS = ["x", "L0_conv_w_qkv", "L0_conv_w_out", "L0_conv_b_out", "L0_ffn_W_gate", "L0_ffn_W1", "L0_ffn_W2"]


def kernel(**inputs):
    import concourse.bacc as bacc
    from concourse.bass_utils import run_bass_kernel_spmd

    nc = bacc.Bacc("TRN2", target_bir_lowering=False, num_devices=1)
    arrays, args = {}, []
    for name in _INS:
        a = np.ascontiguousarray(inputs[name])
        arrays[f"in_{name}"] = a
        args.append(nc.dram_tensor(f"in_{name}", a.shape, mybir.dt.from_np(a.dtype), kind="ExternalInput").ap())
    out = nc.dram_tensor("out_x", (B, C, H, W), F32, kind="ExternalOutput").ap()
    build(nc, *args, out)
    r = run_bass_kernel_spmd(nc, [arrays], core_ids=[0])
    return r.results[0]["out_x"]
```
